# Optimizing a Trainium2 kernel written in Bass

```python
import numpy as np
import jax
import jax.numpy as jnp

def _softmax(x, axis=-1):
    return jax.nn.softmax(x, axis=axis)

def _gelu(x):
    return jax.nn.gelu(x, approximate=True)

def _silu(x):
    return jax.nn.silu(x)

def _sigmoid(x):
    return jax.nn.sigmoid(x)

def _layernorm(x, axis=-1, eps=1e-05):
    m = jnp.mean(x, axis=axis, keepdims=True)
    v = jnp.var(x, axis=axis, keepdims=True)
    return (x - m) / jnp.sqrt(v + eps)

def _scatter_add(tgt, idx, src, axis=0):
    return tgt.at[idx].add(src)

def _segment_sum(src, seg, n):
    return jax.ops.segment_sum(src, seg, n)
kernel_name = 'mk_adaln_d1_jaxref_r8_327db2'

def setup_inputs(seed: int=0):
    np.random.seed(seed)
    _w = jnp.asarray

    def _L0_attn_setup():
        import jax, jax.numpy as jnp
        import numpy as np
        N_HEADS = 16
        PALACE_PERIOD = 8

        def _palace_mask(T, inter_palace_weight):
            idx = jnp.arange(T) % PALACE_PERIOD
            intra = idx[:, None] == idx[None, :]
            w = jax.nn.sigmoid(inter_palace_weight)
            return jnp.where(intra, jnp.float32(1.0), w)
        key = jax.random.key(seed)
        B, T, D = (2, 256, 128)
        x = jax.random.normal(key, (B, T, D), dtype=jnp.float32)
        inter_palace_weight = jnp.array(0.1, dtype=jnp.float32)
        return {'x': x, 'inter_palace_weight': inter_palace_weight}
    _L0_attn_in = _L0_attn_setup()

    def _L0_ffn_setup():
        import jax, jax.numpy as jnp
        import numpy as np
        B, L, D = (2, 256, 128)
        E = 15
        H = D * 1
        K = 3
        T = 1.0
        key = jax.random.key(seed)
        ks = jax.random.split(key, 12)
        s = 0.02
        return {'x': jax.random.normal(ks[0], (B, L, D), dtype=jnp.float32), 'router_W': jax.random.normal(ks[1], (D, E), dtype=jnp.float32) * s, 'router_b': jnp.zeros((E,), dtype=jnp.float32), 'sW1': jax.random.normal(ks[2], (D, H), dtype=jnp.float32) * s, 'sb1': jnp.zeros((H,), dtype=jnp.float32), 'sW2': jax.random.normal(ks[3], (H, D), dtype=jnp.float32) * s, 'sb2': jnp.zeros((D,), dtype=jnp.float32), 'eW1': jax.random.normal(ks[4], (E, D, H), dtype=jnp.float32) * s, 'eb1': jnp.zeros((E, H), dtype=jnp.float32), 'eW2': jax.random.normal(ks[5], (E, H, D), dtype=jnp.float32) * s, 'eb2': jnp.zeros((E, D), dtype=jnp.float32)}
    _L0_ffn_in = _L0_ffn_setup()
    _L0_c = _w((lambda *s: np.random.randn(*s).astype(np.float32) * 0.05)(2, 128))
    _L0_wmod = _w((lambda *s: np.random.randn(*s).astype(np.float32) * 0.05)(128, 6 * 128) * 128 ** (-0.5))
    _d = {'L0_attn_x': _L0_attn_in['x'], 'L0_attn_inter_palace_weight': _L0_attn_in['inter_palace_weight'], 'L0_ffn_router_W': _L0_ffn_in['router_W'], 'L0_ffn_router_b': _L0_ffn_in['router_b'], 'L0_ffn_sW1': _L0_ffn_in['sW1'], 'L0_ffn_sb1': _L0_ffn_in['sb1'], 'L0_ffn_sW2': _L0_ffn_in['sW2'], 'L0_ffn_sb2': _L0_ffn_in['sb2'], 'L0_ffn_eW1': _L0_ffn_in['eW1'], 'L0_ffn_eb1': _L0_ffn_in['eb1'], 'L0_ffn_eW2': _L0_ffn_in['eW2'], 'L0_ffn_eb2': _L0_ffn_in['eb2'], 'L0_c': _L0_c, 'L0_wmod': _L0_wmod}
    _x0 = _d['L0_attn_x']
    _d['L0_attn_x'] = jax.random.normal(jax.random.fold_in(jax.random.key(seed), 1), (2, 1024, 128), dtype=_x0.dtype)
    del _x0
    return _d

def reference(L0_attn_x, L0_attn_inter_palace_weight, L0_ffn_router_W, L0_ffn_router_b, L0_ffn_sW1, L0_ffn_sb1, L0_ffn_sW2, L0_ffn_sb2, L0_ffn_eW1, L0_ffn_eb1, L0_ffn_eW2, L0_ffn_eb2, L0_c, L0_wmod):

    def _L0_attn_ref(x, inter_palace_weight):
        import jax, jax.numpy as jnp
        import numpy as np
        N_HEADS = 16
        PALACE_PERIOD = 8

        def _palace_mask(T, inter_palace_weight):
            idx = jnp.arange(T) % PALACE_PERIOD
            intra = idx[:, None] == idx[None, :]
            w = jax.nn.sigmoid(inter_palace_weight)
            return jnp.where(intra, jnp.float32(1.0), w)
        B, T, D = x.shape
        H = N_HEADS
        hd = D // H
        scale = hd ** (-0.5)
        q = x.reshape(B, T, H, hd).transpose(0, 2, 1, 3)
        scores = jnp.einsum('bhqd,bhkd->bhqk', q, q) * scale
        m = _palace_mask(T, inter_palace_weight)
        attn = jax.nn.softmax(scores * m, axis=-1)
        out = jnp.einsum('bhqk,bhkd->bhqd', attn, q)
        return out.transpose(0, 2, 1, 3).reshape(B, T, D)

    def _L0_ffn_ref(x, router_W, router_b, sW1, sb1, sW2, sb2, eW1, eb1, eW2, eb2):
        import jax, jax.numpy as jnp
        import numpy as np
        B, L, D = (2, 256, 128)
        E = 15
        H = D * 1
        K = 3
        T = 1.0
        b, l, d = x.shape
        n = b * l
        xt = x.reshape(n, d)
        shared = jax.nn.relu(xt @ sW1 + sb1) @ sW2 + sb2
        logits = xt @ router_W + router_b
        probs = jax.nn.softmax(logits / T, axis=-1)
        top_p, top_i = jax.lax.top_k(probs, K)
        cw = jnp.zeros((n, E), dtype=probs.dtype)
        cw = cw.at[jnp.arange(n)[:, None], top_i].set(top_p)
        h = jax.nn.relu(jnp.einsum('nd,edh->neh', xt, eW1) + eb1)
        ye = jnp.einsum('neh,ehd->ned', h, eW2) + eb2
        routed = jnp.einsum('ned,ne->nd', ye, cw)
        return (shared + routed).reshape(b, l, d)
    x = L0_attn_x
    mod = (_silu(L0_c) @ L0_wmod).reshape(L0_c.shape[0], 6, 1, -1)
    sa, ca, ga, sb, cb, gb = (mod[:, 0], mod[:, 1], mod[:, 2], mod[:, 3], mod[:, 4], mod[:, 5])
    ga = (2 * (ga >= 0) - 1) * jnp.maximum(jnp.abs(ga), 0.25)
    gb = (2 * (gb >= 0) - 1) * jnp.maximum(jnp.abs(gb), 0.25)
    h = _layernorm(x, axis=-1) * (1 + ca) + sa
    x = x + ga * _L0_attn_ref(h, L0_attn_inter_palace_weight)
    h = _layernorm(x, axis=-1) * (1 + cb) + sb
    x = x + gb * _L0_ffn_ref(h, L0_ffn_router_W, L0_ffn_router_b, L0_ffn_sW1, L0_ffn_sb1, L0_ffn_sW2, L0_ffn_sb2, L0_ffn_eW1, L0_ffn_eb1, L0_ffn_eW2, L0_ffn_eb2)
    return x

_drawn_inputs = setup_inputs


def setup_inputs(seed=0):
    import zlib

    import numpy as np

    out = dict(_drawn_inputs(seed))
    spreads = {'L0_ffn_router_b': (0.0, 0.8),
     'L0_ffn_sb1': (0.0, 0.8),
     'L0_ffn_sb2': (0.0, 0.287),
     'L0_ffn_eb1': (0.0, 0.8),
     'L0_ffn_eb2': (0.0, 0.8)}
    factors = {'L0_ffn_router_W': 8.0,
     'L0_ffn_sW1': 7.359,
     'L0_ffn_sW2': 5.814,
     'L0_ffn_eW1': 8.0,
     'L0_ffn_eW2': 8.0}
    for name, (base, spread) in spreads.items():
        noise = np.random.default_rng([zlib.crc32(name.encode()), seed]).standard_normal(out[name].shape)
        drawn = base * np.exp(spread * noise) if base else spread * noise
        out[name] = jnp.asarray(drawn.astype(out[name].dtype))
    for name, factor in factors.items():
        out[name] = (out[name] * factor).astype(out[name].dtype)
    return out
```

```python
from contextlib import ExitStack

import concourse.bass as bass
from concourse import mybir

F32 = mybir.dt.float32
BF16 = mybir.dt.bfloat16
I32 = mybir.dt.int32
U32 = mybir.dt.uint32
ALU = mybir.AluOpType
ACT = mybir.ActivationFunctionType
AX = mybir.AxisListType
RMAX = bass.bass_isa.ReduceOp.max

B, T, D = 2, 1024, 128
H, HD = 16, 8
C = 8
M = T // C
E, K = 15, 3
NT = B * T
TILES = B * C
HG = B * H
G = 4
EPS = 1e-5
SCALE = HD ** -0.5
SAFE_EXPONENT = 60.0
PARTS = 3
ROWS = PARTS * PARTS * HD
LOADS = PARTS + 2
KROWS = ROWS + PARTS
STEPS = 2 * C
ITERS = HG // G // 2
SEC = G * C + 1
BODY = 2 * SEC
OUT_AT = 6
SLOTS = 3
CH = 512
HALVES = T // CH
NCH = NT // CH


def adaln_block(nc, x, ipw, router_w, router_b, sw1, sb1, sw2, sb2, ew1, eb1, ew2, eb2, cvec, wmod, out,
                force_exact=False):
    ctx = ExitStack()
    with ctx:
        def sb(name, shape, dt=F32):
            return ctx.enter_context(nc.sbuf_tensor(name, shape, dt))

        def ps(name, shape):
            return ctx.enter_context(nc.psum_tensor(name, shape, F32))

        def sem(name):
            return ctx.enter_context(nc.semaphore(name))

        x_sb = sb("x_sb", [128, C, B * D])
        h_sb = sb("h_sb", [128, C, B * D])
        attn = sb("attn", [128, C, B * D])
        hT = sb("hT", [128, NT])
        hw = sb("hw", [128, T])
        rem = sb("rem", [128, 2, T])
        part = sb("part", [128, B, 2, PARTS, T], BF16)
        keys = [[sb(f"keys{j}{q}", [KROWS, T], BF16) for q in range(G)] for j in range(2)]
        qin = [[sb(f"qin{j}{q}", [KROWS, T], BF16) for q in range(G)] for j in range(2)]
        qout = [[sb(f"qout{j}{q}", [KROWS, T], BF16) for q in range(G)] for j in range(2)]
        val = [sb(f"val{j}", [128, C, G, 32]) for j in range(2)]
        prob = [sb(f"prob{j}", [128, G, T]) for j in range(2)]
        oT = sb("oT", [128, T])
        rden = sb("rden", [128, C, G])
        ident = sb("ident", [128, 128])
        ones = sb("ones", [128, 128])
        spare = sb("spare", [1, 1])
        cT = sb("cT", [128, B])
        sil = sb("sil", [128, 4, B])
        silb = sb("silb", [128, B, 128])
        wm = sb("wm", [128, 6 * D])
        mod = sb("mod", [128, 5, B * D])
        modt = sb("modt", [128, B * D])
        gbT = sb("gbT", [128, 4, B])
        wcol = sb("wcol", [128, 3])
        stats = sb("stats", [128, C, B, 6])
        mv = sb("mv", [128, C, B, 2])
        rstd = sb("rstd", [128, 5, TILES])
        rint = sb("rint", [128, 2, TILES], I32)
        norm2 = sb("norm2", [128, C, HG])
        nmax = sb("nmax", [128, 2])
        flag = sb("flag", [128, 1], I32)
        shift = sb("shift", [128, HG, C])
        shift2 = sb("shift2", [128, HG, C])
        srem = sb("srem", [128, B * 128])
        spart = sb("spart", [128, PARTS, B * 128], BF16)
        rw = sb("rw", [128, E])
        rb = sb("rb", [128, E])
        b1 = [sb(f"b1_{k}", [128, 1]) for k in range(3)]
        b2c = sb("b2c", [128, 3])
        b2r = sb("b2r", [E, D])
        w1 = [sb(f"w1_{k}", [128, D]) for k in range(3)]
        w2 = [sb(f"w2_{k}", [128, D]) for k in range(3)]
        iota = sb("iota", [128, E])
        lg = sb("lg", [128, 4, TILES, E])
        lred = sb("lred", [128, 3, TILES])
        top = sb("top", [128, TILES, 8])
        topi = sb("topi", [128, TILES, 8], U32)
        topf = sb("topf", [128, TILES, 8])
        hid = sb("hid", [128, NCH, CH])
        gat = sb("gat", [128, NCH, CH])
        cwr = part[0:1].rearrange("o b s p t -> o (b s p t)").bitcast(F32).rearrange("o (k t) -> o k t", k=3)
        cwb = [prob[0][:, 0:2, :], prob[0][:, 2:4, :], prob[1][:, 0:2, :]]
        cwT = prob[1][0:E, 2:4, :]

        slot = [ps(f"slot{k}", [128, T]) for k in range(SLOTS)]
        acc = ps("acc", [128, T])

        part_d = nc.dram_tensor("part_d", (2, HG, PARTS, HD, T), BF16, kind="Internal").ap()
        shift_d = nc.dram_tensor("shift_d", (PARTS, HG, T), BF16, kind="Internal").ap()
        cw_d = nc.dram_tensor("cw_d", (E, NT), F32, kind="Internal").ap()

        ld_mod = sem("ld_mod")
        ld_x = sem("ld_x")
        ld_ffn = sem("ld_ffn")
        consts = sem("consts")
        act_exp = sem("act_exp")
        silu_ok = sem("silu_ok")
        mod_mm = sem("mod_mm")
        h_ok = sem("h_ok")
        sq_ok = sem("sq_ok")
        hT_mm = sem("hT_mm")
        hT_ok = sem("hT_ok")
        rem_ok = sem("rem_ok")
        cut_a = sem("cut_a")
        cut_v = sem("cut_v")
        part_wr = sem("part_wr")
        nm_part = sem("nm_part")
        nm_all = sem("nm_all")
        flag_ok = sem("flag_ok")
        ex_ld = sem("ex_ld")
        ex_mm = sem("ex_mm")
        ex_max = sem("ex_max")
        shift_ok = sem("shift_ok")
        shiftT_mm = sem("shiftT_mm")
        spart_ok = sem("spart_ok")
        shift_wr = sem("shift_wr")
        opnd = [sem("opnd0"), sem("opnd1")]
        val_ok = [sem("val_ok0"), sem("val_ok1")]
        filled = sem("filled")
        exp_done = sem("exp_done")
        pv_done = sem("pv_done")
        evac = sem("evac")
        norm_done = sem("norm_done")
        h2T_mm = sem("h2T_mm")
        h2T_ok = sem("h2T_ok")
        logit_mm = sem("logit_mm")
        lsub = sem("lsub")
        lexp = sem("lexp")
        cw_ok = sem("cw_ok")
        cwT_mm = sem("cwT_mm")
        cwT_ok = sem("cwT_ok")
        cw_wr = sem("cw_wr")
        w_ld = [sem(f"w_ld{k}") for k in range(3)]
        row_ld = [sem(f"row_ld{k}") for k in range(3)]
        cwb_ok = sem("cwb_ok")
        l1_done = sem("l1_done")
        hid_ok = sem("hid_ok")
        gat_ok = sem("gat_ok")
        l2_done = sem("l2_done")
        ffn_mm = sem("ffn_mm")
        ffT_ok = sem("ffT_ok")
        y_mm = sem("y_mm")
        y_ok = sem("y_ok")
        out_wr = sem("out_wr")
        dve_seq = sem("dve_seq")
        act_seq = sem("act_seq")
        pool_seq = sem("pool_seq")

        block = ctx.enter_context(nc.Block())

        def fill_count(it, r, first):
            return BODY * it + r + 1 - (0 if first and r < OUT_AT else 1)

        def exp_count(it, units):
            return G * STEPS * it + units

        def pv_count(it, step, half):
            return HALVES * STEPS * it - HALVES + HALVES * step + half + 1

        def evac_count(it, j, half):
            return 2 * HALVES * it - HALVES + HALVES * j + half + 1

        def norm_count(it, j):
            return 2 * it + j

        def uses(first):
            for j in range(2):
                at = 0
                for u in range(G * C):
                    if at == OUT_AT:
                        if not (first and j == 0):
                            yield SEC * j + at, j, None, None
                        at += 1
                    yield SEC * j + at, j, u // G, u % G
                    at += 1

        def unit_at(r):
            j, at = r // SEC, r % SEC
            return G * C * j + at - (1 if at > OUT_AT else 0)

        def exact_wanted(eng):
            eng.wait_ge(flag_ok, 1)
            return eng.value_load(flag[0:1, 0:1], min_val=0, max_val=1)

        @block.sync
        def _(sp):
            with nc.allow_non_contiguous_dma(reason="small transposed vectors"):
                sp.dma_start(cT[:], cvec.rearrange("b d -> d b")).then_inc(ld_mod, 16)
                sp.dma_start(wcol[:, 0:1], ipw.partition_broadcast(128)).then_inc(ld_mod, 16)
                sp.dma_start(wm[:], wmod).then_inc(ld_mod, 16)
                for b in range(B):
                    sp.dma_start(x_sb[:, :, b * D:(b + 1) * D],
                                 x[b].rearrange("(m c) d -> m c d", c=C)).then_inc(ld_x, 16)
                sp.dma_start(rw[:], router_w).then_inc(ld_ffn, 16)
                sp.dma_start(rb[:], router_b.partition_broadcast(128)).then_inc(ld_ffn, 16)
                sp.dma_start(b2c[:, 0:1], sb2.rearrange("(h o) -> h o", o=1)).then_inc(ld_ffn, 16)
                sp.dma_start(b2r[:], eb2).then_inc(ld_ffn, 16)
                sp.dma_start(w1[2][:], sw1).then_inc(w_ld[2], 16)
                sp.dma_start(w2[2][:], sw2).then_inc(w_ld[2], 16)
                sp.dma_start(b1[2][:], sb1.rearrange("(h o) -> h o", o=1)).then_inc(w_ld[2], 16)
                for k in range(2):
                    sp.dma_start(w1[k][:], ew1[k]).then_inc(w_ld[k], 16)
                    sp.dma_start(w2[k][:], ew2[k]).then_inc(w_ld[k], 16)
                    sp.dma_start(b1[k][:], eb1[k].rearrange("(h o) -> h o", o=1)).then_inc(w_ld[k], 16)

            for b in range(B):
                sp.wait_ge(cut_v, 2 * b + 2)
                for s in range(2):
                    for p in range(PARTS):
                        sp.dma_start(part_d[s, b * H:(b + 1) * H, p], part[:, b, s, p]).then_inc(part_wr, 16)
            sp.wait_ge(part_wr, 16 * 2 * B * PARTS)
            sp.wait_ge(consts, 6)

            def load_keys(dst, g, signal):
                for a in range(PARTS):
                    sp.dma_start(dst[PARTS * HD * a:PARTS * HD * (a + 1), :],
                                 part_d[0, g, a].unsqueeze(0).broadcast_to((PARTS, HD, T))).then_inc(signal, 16)

            def load_queries(dst, s, g, signal):
                src = part_d[s, g].rearrange("p d t -> (p d) t")
                sp.dma_start(dst[0:ROWS, :], src.unsqueeze(0).broadcast_to((PARTS, PARTS * HD, T))
                             ).then_inc(signal, 16)

            exact = exact_wanted(sp)
            with sp.If(exact > 0):
                with sp.Fori(0, HG) as g:
                    sp.wait_ge(ex_max, C * g + C)
                    load_keys(keys[0][0], g, ex_ld)
                    load_queries(qin[0][0], 0, g, ex_ld)
                    load_queries(qout[0][0], 1, g, ex_ld)
                sp.wait_ge(ex_max, C * HG + C)

            sp.wait_ge(spart_ok, 1)
            sp.dma_start(shift_d.rearrange("p (b h) (c m) -> p b (h c) m", b=B, c=C).rearrange("p b q m -> q p b m"),
                         spart[:].rearrange("q p (b m) -> q p b m", b=B)).then_inc(shift_wr, 16)
            sp.wait_ge(shift_wr, 16)

            def load_group(it, j):
                for q in range(G):
                    g = 2 * G * it + G * j + q
                    load_keys(keys[j][q], g, opnd[j])
                    load_queries(qin[j][q], 0, g, opnd[j])
                    load_queries(qout[j][q], 1, g, opnd[j])
                    sp.dma_start(qin[j][q][ROWS:KROWS, :], shift_d[:, g]).then_inc(opnd[j], 16)
                    sp.dma_start(qout[j][q][ROWS:KROWS, :], shift_d[:, g]).then_inc(opnd[j], 16)

            for j in range(2):
                load_group(0, j)
            with sp.Fori(1, ITERS) as it:
                for j in range(2):
                    sp.wait_ge(filled, BODY * it + SEC * (j + 1) - 1 - BODY)
                    load_group(it, j)

            sp.wait_ge(cwT_ok, 1)
            sp.dma_start(cw_d, cwT.rearrange("e a t -> e (a t)")).then_inc(cw_wr, 16)
            sp.wait_ge(cw_wr, 16)

            def load_row(e, k):
                sp.dma_start(cwr[0:1, k, :], cw_d[bass.ds(e, 1), :]).then_inc(row_ld[k], 16)

            def load_weights(e, k):
                sp.dma_start(w1[k][:], ew1[e]).then_inc(w_ld[k], 16)
                sp.dma_start(w2[k][:], ew2[e]).then_inc(w_ld[k], 16)
                sp.dma_start(b1[k][:], eb1[e].rearrange("(h o) -> h o", o=1)).then_inc(w_ld[k], 16)

            for k in range(3):
                load_row(k, k)
            sp.wait_ge(l2_done, NCH)
            load_weights(2, 2)
            with sp.Fori(1, E // 3) as i:
                for k in range(3):
                    sp.wait_ge(cwb_ok, 3 * i + k - 2)
                    load_row(3 * i + k, k)
                    sp.wait_ge(l2_done, NCH * (3 * i + k - 1))
                    load_weights(3 * i + k, k)

            out_v = out.rearrange("b (m c) d -> b m c d", c=C)
            for b in range(B):
                sp.wait_ge(y_ok, b + 1)
                sp.dma_start(out_v[b], h_sb[:, :, b * D:(b + 1) * D]).then_inc(out_wr, 16)
            sp.wait_ge(out_wr, 16 * B)

        @block.gpsimd
        def _(pool):
            nc.gpsimd.memset(ones[:], 1.0).then_inc(consts, 1)
            nc.gpsimd.memset(ident[:], 0.0).then_inc(pool_seq, 1)
            pool.wait_ge(pool_seq, 1)
            nc.gpsimd.affine_select(out=ident[:], in_=ident[:], compare_op=ALU.not_equal, fill=1.0, base=0,
                                    pattern=[[-1, 128]], channel_multiplier=1).then_inc(consts, 1)
            nc.gpsimd.iota(iota[:], [[1, E]], base=0, channel_multiplier=0,
                           allow_small_or_imprecise_dtypes=True).then_inc(consts, 1)
            for j in range(2):
                nc.gpsimd.memset(val[j][:], 0.0).then_inc(pool_seq, 1)
            pool.wait_ge(pool_seq, 3)
            for j in range(2):
                last = nc.gpsimd.memset(val[j][:, :, :, HD:HD + 1], 1.0)
            last.then_inc(consts, 1)
            for j in range(2):
                for q in range(G):
                    last = nc.gpsimd.memset(keys[j][q][:], 1.0)
                last.then_inc(consts, 1)

            pool.wait_ge(nm_part, 1)
            nc.gpsimd.partition_all_reduce(nmax[:, 1:2], nmax[:, 0:1], 128, RMAX).then_inc(nm_all, 1)

            def copy_values(it, j):
                at = 2 * G * HD * it + G * HD * j
                nc.gpsimd.tensor_copy(val[j][:, :, :, 0:HD],
                                      h_sb[:, :, bass.ds(at, G * HD)].rearrange("m c (q d) -> m c q d", q=G)
                                      ).then_inc(val_ok[j], 1)

            pool.wait_ge(h_ok, 1)
            pool.wait_ge(consts, 6)
            for j in range(2):
                copy_values(0, j)
            with pool.Fori(1, ITERS) as it:
                for j in range(2):
                    pool.wait_ge(pv_done, pv_count(it, C * j - C if j == 0 else 0, HALVES - 1))
                    copy_values(it, j)

            def spread(i, k):
                pool.wait_ge(row_ld[k], 16 * i + 16)
                pool.wait_ge(pool_seq, 3 * i + k + 3)
                nc.gpsimd.tensor_tensor(spare[:], ones[0:1, 0:1], ones[0:1, 0:1], ALU.mult).then_inc(pool_seq, 1)
                nc.gpsimd.partition_broadcast(cwb[k].rearrange("p a t -> p (a t)"), cwr[0:1, k, :],
                                              128).then_inc(cwb_ok, 1)

            for k in range(3):
                spread(0, k)
            with pool.Fori(1, E // 3) as i:
                for k in range(3):
                    pool.wait_ge(gat_ok, NCH * (3 * i + k - 1))
                    spread(i, k)

        @block.scalar
        def _(act):
            seq = [0]

            def link(ins):
                seq[0] += 1
                ins.then_inc(act_seq, 1)
                act.wait_ge(act_seq, seq[0])

            act.wait_ge(ld_mod, 48)
            nc.scalar.activation(sil[:, 0], cT[:], ACT.Exp, scale=-1.0).then_inc(act_exp, 1)
            nc.scalar.activation(wcol[:, 1:2], wcol[:, 0:1], ACT.Exp, scale=-1.0).then_inc(act_exp, 1)

            act.wait_ge(h_ok, 1)
            nc.scalar.activation(attn[:], h_sb[:], ACT.Square).then_inc(sq_ok, 1)
            for b in range(B):
                act.wait_ge(hT_mm, b + 1)
                act.wait_ge(silu_ok, 3)
                nc.scalar.activation(hT[:, b * T:(b + 1) * T], slot[b][:], ACT.Copy).then_inc(hT_ok, 1)
                if b:
                    act.wait_ge(cut_v, 2 * b)
                link(nc.scalar.activation(hw[:], slot[b][:], ACT.Copy, scale=wcol[:, 2:3]))
                nc.scalar.activation(part[:, b, 1, 0], hw[:], ACT.Copy).then_inc(cut_a, 1)
                act.wait_ge(rem_ok, b + 1)
                nc.scalar.activation(part[:, b, 1, 1], rem[:, 1], ACT.Copy).then_inc(cut_a, 1)

            def exps(it, first):
                for r, j, c, q in uses(first):
                    if c is None:
                        continue
                    step = C * j + c
                    act.wait_ge(filled, fill_count(it, r, first))
                    if q == 0 and not (first and step < 2):
                        act.wait_ge(pv_done, pv_count(it, step - 1, HALVES - 1))
                    nc.scalar.activation(prob[c % 2][:, q, :], slot[r % SLOTS][:], ACT.Exp,
                                         scale=SCALE).then_inc(exp_done, 1)

            exps(0, True)
            with act.Fori(1, ITERS) as it:
                exps(it, False)

            for b in range(B):
                act.wait_ge(h2T_mm, b + 1)
                nc.scalar.activation(hT[:, b * T:(b + 1) * T], slot[b][:], ACT.Copy).then_inc(h2T_ok, 1)
            act.wait_ge(lsub, 1)
            nc.scalar.activation(lg[:, 1], lg[:, 0], ACT.Exp).then_inc(lexp, 1)
            act.wait_ge(cwT_mm, 1)
            nc.scalar.activation(cwT[:, 0, :], slot[0][0:E, :], ACT.Copy)
            nc.scalar.activation(cwT[:, 1, :], slot[1][0:E, :], ACT.Copy).then_inc(cwT_ok, 1)

            def hidden(e, n0, bias):
                for q in range(NCH):
                    act.wait_ge(l1_done, n0 + q + 1)
                    if e is not None:
                        act.wait_ge(gat_ok, n0 + q + 1 - NCH)
                    nc.scalar.activation(hid[:, q], slot[q // 2][:, (q % 2) * CH:(q % 2 + 1) * CH],
                                         ACT.Relu, bias=bias).then_inc(hid_ok, 1)

            hidden(None, 0, b1[2][:])
            with act.Fori(0, E // 3) as i:
                for k in range(3):
                    hidden(k, NCH * (3 * i + k + 1), b1[k][:])

            act.wait_ge(ffn_mm, 1)
            for q in range(NCH):
                b = q // 2
                act.wait_ge(gat_ok, NCH * (E + 1))
                src = (slot[2], acc)[q // 2][:, (q % 2) * CH:(q % 2 + 1) * CH]
                nc.scalar.activation(hT[:, q * CH:(q + 1) * CH], src, ACT.Identity,
                                     bias=gbT[:, 3, b:b + 1], scale=gbT[:, 2, b:b + 1]).then_inc(ffT_ok, 1)

        @block.vector
        def _(dve):
            seq = [0]
            v = nc.vector

            def link(ins):
                seq[0] += 1
                ins.then_inc(dve_seq, 1)
                dve.wait_ge(dve_seq, seq[0])

            dve.wait_ge(act_exp, 2)
            link(v.tensor_scalar(sil[:, 1], sil[:, 0], 1.0, None, ALU.add))
            link(v.reciprocal(sil[:, 2], sil[:, 1]))
            link(v.tensor_tensor(sil[:, 3], sil[:, 2], cT[:], ALU.mult))
            dve.wait_ge(consts, 2)
            for b in range(B):
                v.tensor_scalar(silb[:, b], ones[:], sil[:, 3, b:b + 1], None, ALU.mult).then_inc(silu_ok, 1)
            link(v.tensor_scalar(wcol[:, 1:2], wcol[:, 1:2], 1.0, None, ALU.add))
            v.reciprocal(wcol[:, 2:3], wcol[:, 1:2]).then_inc(silu_ok, 1)

            def normalise(src):
                for c in range(C):
                    for b in range(B):
                        last = v.bn_stats(stats[:, c, b], src[:, c, b * D:(b + 1) * D])
                link(last)
                for c in range(C):
                    for b in range(B):
                        last = v.bn_aggr(mv[:, c, b], stats[:, c, b])
                link(last)
                var, y, t = rstd[:, 0], rstd[:, 1], rstd[:, 2]
                link(v.tensor_scalar(var, mv[:, :, :, 1].rearrange("p c b -> p (c b)"), EPS, None, ALU.add))
                link(v.tensor_scalar(rint[:, 0], var.bitcast(I32), 1, None, ALU.logical_shift_right))
                link(v.tensor_scalar(rint[:, 1], rint[:, 0], -1.0, float(0x5F3759DF), ALU.mult, ALU.add))
                link(v.tensor_copy(y, rint[:, 1].bitcast(F32)))
                for _ in range(4):
                    link(v.tensor_tensor(t, y, y, ALU.mult))
                    link(v.scalar_tensor_tensor(t, t, -0.5, var, ALU.mult, ALU.mult))
                    link(v.scalar_tensor_tensor(y, t, 1.5, y, ALU.add, ALU.mult))
                for c in range(C):
                    for b in range(B):
                        last = v.tensor_scalar(h_sb[:, c, b * D:(b + 1) * D], src[:, c, b * D:(b + 1) * D],
                                               mv[:, c, b, 0:1], y[:, B * c + b:B * c + b + 1],
                                               ALU.subtract, ALU.mult)
                link(last)

            def over_classes(row):
                return row.unsqueeze(1).broadcast_to((128, C, B * D))

            def modulate(add_row, mul_row):
                link(v.tensor_tensor(h_sb[:], h_sb[:], over_classes(mod[:, mul_row]), ALU.mult))
                return v.tensor_tensor(h_sb[:], h_sb[:], over_classes(mod[:, add_row]), ALU.add)

            def gate(dst, tmp):
                link(v.tensor_scalar(tmp, dst, -1.0, 0.25, ALU.mult, ALU.max))
                link(v.tensor_tensor(tmp, tmp, dst, ALU.max))
                link(v.tensor_scalar(dst, dst, 0.0, 2.0, ALU.is_ge, ALU.mult))
                link(v.scalar_tensor_tensor(dst, dst, -1.0, tmp, ALU.add, ALU.mult))

            dve.wait_ge(ld_x, 32)
            normalise(x_sb)
            dve.wait_ge(mod_mm, 1)
            for b in range(B):
                cols = slice(b * D, (b + 1) * D)
                for k in range(5):
                    src = slot[b][:, k * D:(k + 1) * D]
                    if k in (1, 4):
                        last = v.tensor_scalar(mod[:, k, cols], src, 1.0, None, ALU.add)
                    else:
                        last = v.tensor_copy(mod[:, k, cols], src)
            link(last)
            link(v.tensor_copy(gbT[:, 0], slot[2][:, 0:B]))
            modulate(0, 1).then_inc(h_ok, 1)

            for b in range(B):
                src = hT[:, b * T:(b + 1) * T]
                dve.wait_ge(hT_ok, b + 1)
                link(v.tensor_copy(part[:, b, 0, 0], src))
                dve.wait_ge(cut_a, 2 * b + 1)
                v.tensor_tensor(rem[:, 1], hw[:], part[:, b, 1, 0], ALU.subtract).then_inc(rem_ok, 1)
                link(v.tensor_tensor(rem[:, 0], src, part[:, b, 0, 0], ALU.subtract))
                link(v.tensor_copy(part[:, b, 0, 1], rem[:, 0]))
                v.tensor_tensor(part[:, b, 0, 2], rem[:, 0], part[:, b, 0, 1], ALU.subtract).then_inc(cut_v, 1)
                dve.wait_ge(cut_a, 2 * b + 2)
                v.tensor_tensor(part[:, b, 1, 2], rem[:, 1], part[:, b, 1, 1], ALU.subtract).then_inc(cut_v, 1)

            dve.wait_ge(sq_ok, 1)
            link(v.tensor_reduce(norm2[:].rearrange("p c g -> p (c g)"),
                                 attn[:].rearrange("p c (g d) -> p (c g) d", d=HD), AX.X, ALU.add))
            v.tensor_reduce(nmax[:, 0:1], norm2[:].rearrange("p c g -> p (c g)"), AX.X, ALU.max
                            ).then_inc(nm_part, 1)
            dve.wait_ge(nm_all, 1)
            link(v.tensor_scalar(shift[:].rearrange("p g c -> p c g"), norm2[:], nmax[:, 1:2], -0.5,
                                 ALU.add, ALU.mult))
            limit = -1.0 if force_exact else SAFE_EXPONENT / SCALE
            v.tensor_scalar(flag[:], nmax[:, 1:2], limit, None, ALU.is_gt).then_inc(flag_ok, 1)

            exact = exact_wanted(dve)
            with dve.If(exact > 0):
                dve.sem_inc(ex_max, C)
                with dve.Fori(0, HG) as g:
                    for c in range(C):
                        dve.wait_ge(ex_mm, C * g + c + 1)
                        v.reduce_max(shift[:].rearrange("p g c -> p (g c)")[:, bass.ds(C * g + c, 1)],
                                     slot[c % 2][:], AX.X, negate=True).then_inc(ex_max, 1)
                dve.wait_ge(ex_max, C * HG + C)
            v.tensor_copy(shift2[:], shift[:]).then_inc(shift_ok, 1)

            dve.wait_ge(shiftT_mm, 1)
            sT = acc[:, 0:B * 128]
            link(v.tensor_copy(spart[:, 0], sT))
            link(v.tensor_tensor(srem[:], sT, spart[:, 0], ALU.subtract))
            link(v.tensor_copy(spart[:, 1], srem[:]))
            v.tensor_tensor(spart[:, 2], srem[:], spart[:, 1], ALU.subtract).then_inc(spart_ok, 1)

            gate(mod[:, 2], modt[:])
            gate(gbT[:, 0], gbT[:, 1])
            dve.wait_ge(ld_ffn, 64)
            link(v.tensor_copy(gbT[:, 2], gbT[:, 0]))
            link(v.tensor_scalar(gbT[:, 3], gbT[:, 0], b2c[:, 0:1], None, ALU.mult))

            def take_sums(it, j, tail=False):
                for half in range(HALVES):
                    dve.wait_ge(pv_done, pv_count(it, C * j, half))
                    v.tensor_copy(oT[:, half * CH:(half + 1) * CH],
                                  acc[:, half * CH:(half + 1) * CH]).then_inc(evac, 1)

            def divide(it, j, r, first, chain):
                dve.wait_ge(filled, fill_count(it, r, first))
                sums = slot[r % SLOTS][:].rearrange("m (c q k) -> m c q k", c=C, q=G)
                v.reciprocal(rden[:], sums[:, :, :, HD]).then_inc(dve_seq, 1)
                dve.wait_ge(dve_seq, chain)
                at = 2 * G * HD * it + G * HD * (j - 1)
                v.tensor_tensor(attn[:, :, bass.ds(at, G * HD)].rearrange("m c (q d) -> m c q d", q=G),
                                sums[:, :, :, 0:HD], rden[:].unsqueeze(3).broadcast_to((128, C, G, HD)),
                                ALU.mult).then_inc(norm_done, 1)

            base = seq[0]
            take_sums(0, 1)
            divide(0, 1, SEC + OUT_AT, True, base + 1)
            with dve.Fori(1, ITERS) as it:
                for j in range(2):
                    take_sums(it, j)
                    divide(it, j, SEC * j + OUT_AT, False, 2 * it + (base + j))
            take_sums(ITERS, 0)
            divide(ITERS, 0, 0, False, base + 2 * ITERS)
            seq[0] = base + 2 * ITERS

            dve.wait_ge(norm_done, 2 * ITERS)
            link(v.tensor_tensor(attn[:], attn[:], over_classes(mod[:, 2]), ALU.mult))
            link(v.tensor_tensor(attn[:], attn[:], x_sb[:], ALU.add))
            normalise(attn)
            modulate(3, 4).then_inc(h_ok, 1)

            dve.wait_ge(logit_mm, 1)
            lv = slot[2][:, 0:16 * TILES].rearrange("p (t e) -> p t e", e=16)[:, :, 0:E]

            def over_tiles(row):
                return row.unsqueeze(1).broadcast_to((128, TILES, E))

            def over_experts(col):
                return col.unsqueeze(2).broadcast_to((128, TILES, E))

            link(v.tensor_tensor(lg[:, 0], lv, over_tiles(rb[:]), ALU.add))
            link(v.reduce_max(lred[:, 0], lg[:, 0], AX.X))
            v.tensor_tensor(lg[:, 0], lg[:, 0], over_experts(lred[:, 0]), ALU.subtract).then_inc(lsub, 1)
            dve.wait_ge(lexp, 1)
            link(v.tensor_reduce(lred[:, 1], lg[:, 1], AX.X, ALU.add))
            link(v.reciprocal(lred[:, 2], lred[:, 1]))
            link(v.tensor_tensor(lg[:, 0], lg[:, 1], over_experts(lred[:, 2]), ALU.mult))
            for t in range(TILES):
                last = v.max(top[:, t], lg[:, 0, t])
            link(last)
            for t in range(TILES):
                last = v.max_index(topi[:, t], top[:, t], lg[:, 0, t])
            link(last)
            link(v.tensor_copy(topf[:], topi[:]))
            link(v.tensor_tensor(lg[:, 1], over_tiles(iota[:]), over_experts(topf[:, :, 0]), ALU.is_equal))
            for k in range(1, K):
                link(v.tensor_tensor(lg[:, 2], over_tiles(iota[:]), over_experts(topf[:, :, k]), ALU.is_equal))
                link(v.tensor_tensor(lg[:, 1], lg[:, 1], lg[:, 2], ALU.add))
            v.tensor_tensor(lg[:, 3], lg[:, 0], lg[:, 1], ALU.mult).then_inc(cw_ok, 1)

            for q in range(NCH):
                dve.wait_ge(hid_ok, q + 1)
                v.tensor_copy(gat[:, q], hid[:, q]).then_inc(gat_ok, 1)
            with dve.Fori(0, E // 3) as i:
                for k in range(3):
                    dve.wait_ge(cwb_ok, 3 * i + k + 1)
                    for q in range(NCH):
                        n = NCH * (3 * i + k + 1) + q
                        dve.wait_ge(hid_ok, n + 1)
                        dve.wait_ge(l2_done, n + 1 - NCH)
                        v.tensor_tensor(gat[:, q], hid[:, q], cwb[k][:, q // 2, (q % 2) * CH:(q % 2 + 1) * CH],
                                        ALU.mult).then_inc(gat_ok, 1)

            for b in range(B):
                dve.wait_ge(y_mm, b + 1)
                v.tensor_tensor(h_sb[:, :, b * D:(b + 1) * D], attn[:, :, b * D:(b + 1) * D],
                                slot[b][:].rearrange("m (c d) -> m c d", c=C), ALU.add).then_inc(y_ok, 1)

        @block.tensor
        def _(pe):
            mm = nc.tensor.matmul
            pe.wait_ge(ld_mod, 48)
            pe.wait_ge(silu_ok, 2)
            for b in range(B):
                mm(slot[b][:, 0:CH], silb[:, b], wm[:, 0:CH], start=True, stop=True)
                mm(slot[b][:, CH:5 * D], silb[:, b], wm[:, CH:5 * D], start=True, stop=True)
            mm(slot[2][:, 0:B], wm[:, 5 * D:6 * D], sil[:, 3], start=True, stop=True).then_inc(mod_mm, 1)
            pe.wait_ge(h_ok, 1)
            pe.wait_ge(consts, 2)
            for b in range(B):
                for c in range(C):
                    last = nc.tensor.transpose(slot[b][:, c * M:(c + 1) * M], h_sb[:, c, b * D:(b + 1) * D], ident[:])
                last.then_inc(hT_mm, 1)

            def scores(dst, j, q, c, rows):
                k_c = keys[j][q][0:rows, c * M:(c + 1) * M]
                for half in range(HALVES):
                    lo, hi = half * CH, (half + 1) * CH
                    cuts = [(lo, hi, qout)]
                    if lo <= c * M < hi:
                        cuts = [(lo, c * M, qout), (c * M, (c + 1) * M, qin), ((c + 1) * M, hi, qout)]
                    for a, z, src in cuts:
                        if z > a:
                            last = mm(dst[:, a:z], k_c, src[j][q][0:rows, a:z], start=True, stop=True)
                return last

            exact = exact_wanted(pe)
            with pe.If(exact > 0):
                pe.wait_ge(cut_a, 2 * B)
                with pe.Fori(0, HG) as g:
                    pe.wait_ge(ex_ld, 16 * LOADS * (g + 1))
                    for c in range(C):
                        pe.wait_ge(ex_max, C * g + c + C - 1)
                        scores(slot[c % 2], 0, 0, c, ROWS).then_inc(ex_mm, 1)
                pe.wait_ge(ex_max, C * HG + C)

            pe.wait_ge(shift_ok, 1)
            for b in range(B):
                last = nc.tensor.transpose(acc[:, b * 128:(b + 1) * 128],
                                           shift2[:, b * H:(b + 1) * H].rearrange("p h c -> p (h c)"), ident[:])
            last.then_inc(shiftT_mm, 1)

            def weigh(jv, buf, half, start, stop):
                for q in range(G):
                    last = mm(acc[32 * q:32 * q + 32, half * CH:(half + 1) * CH], val[jv][:, buf[1], q, :],
                              prob[buf[0]][:, q, half * CH:(half + 1) * CH], start=start, stop=stop,
                              tile_position=(0, 32 * q))
                last.then_inc(pv_done, 1)

            def turn_output(r):
                for c in range(C):
                    last = nc.tensor.transpose(slot[r % SLOTS][:, c * M:(c + 1) * M], oT[:, c * M:(c + 1) * M], ident[:])
                last.then_inc(filled, 1)

            def free_slot(it, r, first):
                p = r - SLOTS
                if p < 0 and first:
                    return
                if p >= 0 and p % SEC == OUT_AT and not (first and p < SEC):
                    pe.wait_ge(norm_done, norm_count(it, p // SEC))
                    return
                pe.wait_ge(exp_done, exp_count(it, unit_at(p) + 1 if p >= 0 else p + 1))

            def attend(it, first):
                for r, j, c, q in uses(first):
                    free_slot(it, r, first)
                    if c is None:
                        pe.wait_ge(evac, evac_count(it, j, HALVES - 1))
                        turn_output(r)
                        continue
                    if c == 0 and q == 0:
                        pe.wait_ge(opnd[j], 16 * (LOADS + 2) * G * (it + 1))
                    scores(slot[r % SLOTS], j, q, c, KROWS).then_inc(filled, 1)
                    step = C * j + c
                    if q % 2 == 1 and not (first and step == 0):
                        half, cp, jp = q // 2, (c - 1) % C, j if c else 1 - j
                        if half == 0:
                            pe.wait_ge(exp_done, exp_count(it, G * step))
                            if cp == 0:
                                pe.wait_ge(val_ok[jp], it + 1)
                        if cp == 0 and not (first and j == 0):
                            pe.wait_ge(evac, evac_count(it, j, half))
                        weigh(jp, (cp % 2, cp), half, cp == 0, cp == C - 1)

            pe.wait_ge(cut_a, 2 * B)
            pe.wait_ge(spart_ok, 1)
            attend(0, True)
            with pe.Fori(1, ITERS) as it:
                attend(it, False)
            pe.wait_ge(exp_done, exp_count(ITERS, 0))
            for half in range(HALVES):
                weigh(1, ((C - 1) % 2, C - 1), half, False, True)
            pe.wait_ge(evac, evac_count(ITERS, 0, HALVES - 1))
            turn_output(0)

            pe.wait_ge(h_ok, 2)
            for b in range(B):
                for c in range(C):
                    last = nc.tensor.transpose(slot[b][:, c * M:(c + 1) * M], h_sb[:, c, b * D:(b + 1) * D], ident[:])
                last.then_inc(h2T_mm, 1)
            pe.wait_ge(h2T_ok, B)
            pe.wait_ge(ld_ffn, 64)
            for c in range(C):
                for b in range(B):
                    t = B * c + b
                    last = mm(slot[2][:, 16 * t:16 * t + E], hT[:, b * T + c * M:b * T + (c + 1) * M], rw[:],
                              start=True, stop=True)
            last.then_inc(logit_mm, 1)
            pe.wait_ge(cw_ok, 1)
            for b in range(B):
                for c in range(C):
                    last = nc.tensor.transpose(slot[b][0:E, c * M:(c + 1) * M], lg[:, 3, B * c + b], ident[:])
            last.then_inc(cwT_mm, 1)
            pe.wait_ge(cwT_ok, 1)

            osum = [slot[2][:, 0:CH], slot[2][:, CH:T], acc[:, 0:CH], acc[:, CH:T]]

            def up(k, q, n, fresh=False):
                if not fresh:
                    pe.wait_ge(hid_ok, n + 1 - NCH)
                mm(slot[q // 2][:, (q % 2) * CH:(q % 2 + 1) * CH], w1[k][:], hT[:, q * CH:(q + 1) * CH],
                   start=True, stop=True).then_inc(l1_done, 1)

            def down(k, q, n, start=False):
                pe.wait_ge(gat_ok, n + 1)
                mm(osum[q], w2[k][:], gat[:, q], start=start, stop=False).then_inc(l2_done, 1)

            pe.wait_ge(w_ld[2], 48)
            for q in range(NCH):
                up(2, q, q, fresh=True)
                if q >= 2:
                    down(2, q - 2, q - 2, start=True)
            for q in range(2, NCH):
                down(2, q, q, start=True)
            with pe.Fori(0, E // 3) as i:
                for k in range(3):
                    pe.wait_ge(w_ld[k], 48 * i + (96 if k == 2 else 48))
                    for q in range(NCH):
                        n = NCH * (3 * i + k + 1) + q
                        up(k, q, n)
                        if q >= 2:
                            down(k, q - 2, n - 2)
                    for q in range(2, NCH):
                        down(k, q, NCH * (3 * i + k + 1) + q)
            for q in range(NCH):
                last = mm(osum[q], b2r[:], cwT[:, q // 2, (q % 2) * CH:(q % 2 + 1) * CH], start=False, stop=True)
            last.then_inc(ffn_mm, 1)
            for b in range(B):
                pe.wait_ge(ffT_ok, 2 * b + 2)
                for c in range(C):
                    last = nc.tensor.transpose(slot[b][:, c * M:(c + 1) * M],
                                               hT[:, b * T + c * M:b * T + (c + 1) * M], ident[:])
                last.then_inc(y_mm, 1)


_INS = ["L0_attn_x", "L0_attn_inter_palace_weight", "L0_ffn_router_W", "L0_ffn_router_b", "L0_ffn_sW1",
        "L0_ffn_sb1", "L0_ffn_sW2", "L0_ffn_sb2", "L0_ffn_eW1", "L0_ffn_eb1", "L0_ffn_eW2", "L0_ffn_eb2",
        "L0_c", "L0_wmod"]


def kernel(**inputs):
    import numpy as np
    import concourse.bacc as bacc
    from concourse.bass_utils import run_bass_kernel_spmd

    nc = bacc.Bacc("TRN2", target_bir_lowering=False, num_devices=1)
    arrays, args = {}, []
    for name in _INS:
        a = np.ascontiguousarray(inputs[name])
        if a.ndim == 0:
            a = a.reshape(1)
        arrays[f"in_{name}"] = a
        args.append(nc.dram_tensor(f"in_{name}", a.shape, mybir.dt.from_np(a.dtype), kind="ExternalInput").ap())
    out = nc.dram_tensor("out", (B, T, D), F32, kind="ExternalOutput").ap()
    adaln_block(nc, *args, out)
    r = run_bass_kernel_spmd(nc, [arrays], core_ids=[0])
    return r.results[0]["out"]
```

```python
from contextlib import ExitStack

import concourse.bass as bass
from concourse import mybir

F32 = mybir.dt.float32
BF16 = mybir.dt.bfloat16
I32 = mybir.dt.int32
U32 = mybir.dt.uint32
ALU = mybir.AluOpType
ACT = mybir.ActivationFunctionType
AX = mybir.AxisListType
RMAX = bass.bass_isa.ReduceOp.max

B, T, D = 2, 1024, 128
H, HD = 16, 8
C = 8
M = T // C
E, K = 15, 3
NT = B * T
TILES = B * C
HG = B * H
G = 4
EPS = 1e-5
SCALE = HD ** -0.5
SAFE_EXPONENT = 60.0
ROUNDING = 1.001
PARTS = 3
ROWS = PARTS * PARTS * HD
KROWS = ROWS + PARTS
KEY_LOADS, QUERY_LOADS, SHIFT_LOADS = PARTS * PARTS, PARTS, 2
STEPS = 2 * C
ITERS = HG // G // 2
SEC = G * C + 1
BODY = 2 * SEC
OUT_AT = 6
H2T_AT, LOGIT_AT, CWT_AT = 12, 20, SEC + 18
SLOTS = 3
CH = 512
HALVES = T // CH
FCH = T // CH
FALL = FCH * (E + 1)
UPB = 3
RING = 6


def adaln_block(nc, x, ipw, router_w, router_b, sw1, sb1, sw2, sb2, ew1, eb1, ew2, eb2, cvec, wmod, out,
                force_exact=False):
    ctx = ExitStack()
    with ctx:
        def sb(name, shape, dt=F32):
            return ctx.enter_context(nc.sbuf_tensor(name, shape, dt))

        def ps(name, shape):
            return ctx.enter_context(nc.psum_tensor(name, shape, F32))

        def sem(name):
            return ctx.enter_context(nc.semaphore(name))

        x_sb = sb("x_sb", [128, C, B * D])
        h_sb = sb("h_sb", [128, C, B * D])
        attn = sb("attn", [128, C, B * D])
        hT = sb("hT", [128, NT])
        hw = sb("hw", [128, T])
        rem = sb("rem", [128, 2, T])
        part = sb("part", [128, B, PARTS, 2, T], BF16)
        keys = [sb(f"keys{j}", [KROWS, G, T], BF16) for j in range(2)]
        qry = [sb(f"qry{j}", [KROWS, G, 2, T], BF16) for j in range(2)]
        val = [sb(f"val{j}", [128, C, G, 32]) for j in range(2)]
        prob = [sb(f"prob{j}", [128, G, T]) for j in range(2)]
        oT = sb("oT", [128, T])
        rden = sb("rden", [128, C, G])
        ident = sb("ident", [128, 128])
        ones = sb("ones", [128, 128])
        spare = sb("spare", [1, 1])
        cT = sb("cT", [128, B])
        sil = sb("sil", [128, 4, B])
        silb = sb("silb", [128, B, 128])
        wm = sb("wm", [128, 6 * D])
        mod = sb("mod", [128, 5, B * D])
        modt = sb("modt", [128, B * D])
        gbT = sb("gbT", [128, 4, B])
        wcol = sb("wcol", [128, 3])
        stats = sb("stats", [128, C, 6])
        mv = sb("mv", [128, B, C, 2])
        rstd = sb("rstd", [128, B, 3, C])
        rint = sb("rint", [128, B, 2, C], I32)
        reach = sb("reach", [128, 8])
        flag = sb("flag", [128, 1], I32)
        shift = sb("shift", [128, HG, C])
        srem = sb("srem", [128, B * 128])
        spart1 = sb("spart1", [128, PARTS], BF16)
        spart = sb("spart", [128, PARTS, B * 128], BF16)
        rw = sb("rw", [128, E])
        rb = sb("rb", [128, E])
        b1 = [sb(f"b1_{k}", [128, 1]) for k in range(3)]
        b2c = sb("b2c", [128, 3])
        b2r = sb("b2r", [E, D])
        w1 = [sb(f"w1_{k}", [128, D]) for k in range(3)]
        w2 = [sb(f"w2_{k}", [128, D]) for k in range(3)]
        iota = sb("iota", [128, E])
        lg = sb("lg", [128, B, 4, C, E])
        lred = sb("lred", [128, B, 3, C])
        top = sb("top", [128, B, C, 8])
        topi = sb("topi", [128, B, C, 8], U32)
        topf = sb("topf", [128, B, C, 8])
        ws1 = sb("ws1", [128, D])
        ws2 = sb("ws2", [128, D])
        bs1 = sb("bs1", [128, 1])
        free = part[:].rearrange("p b a s t -> p (b a s t)").bitcast(F32)
        cwb = [free[:, k * T:(k + 1) * T] for k in range(3)]
        cwr = [free[0:1, (3 + k) * T:(4 + k) * T] for k in range(3)]
        cwT = rem[0:E]
        hid = prob[0][:].rearrange("p q (a t) -> p (q a) t", t=CH)
        gat = prob[1][:].rearrange("p q (a t) -> p (q a) t", t=CH)

        slot = [ps(f"slot{k}", [128, T]) for k in range(SLOTS)]
        acc = ps("acc", [128, T])

        up_bank = [slot[0][:, 0:CH], slot[0][:, CH:T], slot[1][:, 0:CH]]

        part_d = nc.dram_tensor("part_d", (HG, PARTS, HD, 2, T), BF16, kind="Internal").ap()
        shift_d = nc.dram_tensor("shift_d", (PARTS, HG, T), BF16, kind="Internal").ap()
        cw_d = nc.dram_tensor("cw_d", (B, E, T), F32, kind="Internal").ap()

        ld_mod = sem("ld_mod")
        ld_x = [sem("ld_x0"), sem("ld_x1")]
        ld_ffn = sem("ld_ffn")
        consts = sem("consts")
        act_exp = sem("act_exp")
        silu_ok = sem("silu_ok")
        mod_mm = sem("mod_mm")
        h_ok = sem("h_ok")
        hT_mm = sem("hT_mm")
        hT_ok = sem("hT_ok")
        rem_ok = sem("rem_ok")
        cut_a = sem("cut_a")
        cut_v = sem("cut_v")
        part_wr = [sem("part_wr0"), sem("part_wr1")]
        flag_ok = sem("flag_ok")
        ex_ld = sem("ex_ld")
        ex_mm = sem("ex_mm")
        ex_max = sem("ex_max")
        ex_seq = sem("ex_seq")
        mod_used = sem("mod_used")
        shiftT_mm = sem("shiftT_mm")
        spart_ok = sem("spart_ok")
        shift_wr = sem("shift_wr")
        opnd = [sem("opnd0"), sem("opnd1")]
        val_ok = [sem("val_ok0"), sem("val_ok1")]
        filled = sem("filled")
        exp_done = sem("exp_done")
        pv_done = sem("pv_done")
        evac = sem("evac")
        norm_done = sem("norm_done")
        h2T_mm = sem("h2T_mm")
        h2T_ok = sem("h2T_ok")
        logit_mm = sem("logit_mm")
        lsub = sem("lsub")
        lexp = sem("lexp")
        cw_ok = sem("cw_ok")
        cwT_mm = sem("cwT_mm")
        cwT_ok = sem("cwT_ok")
        cw_wr = sem("cw_wr")
        w_ld = [sem(f"w_ld{k}") for k in range(3)]
        row_ld = [sem(f"row_ld{k}") for k in range(3)]
        cwb_ok = sem("cwb_ok")
        l1_done = sem("l1_done")
        hid_ok = sem("hid_ok")
        gat_ok = sem("gat_ok")
        l2_done = sem("l2_done")
        ffn_mm = sem("ffn_mm")
        ffT_ok = sem("ffT_ok")
        y_mm = sem("y_mm")
        y_ok = sem("y_ok")
        out_wr = sem("out_wr")
        dve_seq = sem("dve_seq")
        act_seq = sem("act_seq")
        pool_seq = sem("pool_seq")

        block = ctx.enter_context(nc.Block())

        def uses(last=False, first=False):
            extra = {H2T_AT: "h2T", LOGIT_AT: "logit", CWT_AT: "cwT"} if last else {}
            told = []
            for j in range(2):
                section = [("score", j, u // G, u % G) for u in range(G * C)]
                section.insert(OUT_AT, ("none" if first and j == 0 else "turn", j, 0, 0))
                told += section
            for at in sorted(extra):
                told.insert(at, (extra[at], 0, 0, 0))
            return told

        FIRST, MIDDLE, LAST = uses(first=True), uses(), uses(last=True)

        def fill_count(it, r, body):
            return BODY * it - (0 if body is FIRST else 1) + sum(u[0] != "none" for u in body[:r + 1])

        def exp_count(it, units):
            return G * STEPS * it + units

        def pv_count(it, step, half):
            return HALVES * STEPS * it - HALVES + HALVES * step + half + 1

        def evac_count(it, j, half):
            return 2 * HALVES * it - HALVES + HALVES * j + half + 1

        def norm_count(it, j):
            return 2 * it + j

        def chunk(b, m, q):
            return FALL * b + FCH * m + q

        def exact_wanted(eng):
            eng.wait_ge(flag_ok, 1)
            return eng.value_load(flag[0:1, 0:1], min_val=0, max_val=1)

        def cols(b):
            return slice(b * D, (b + 1) * D)

        def experts(eng, b, lo, hi, work):
            if hi - lo > 1:
                with eng.Fori(lo, hi) as i:
                    for k in range(3):
                        work(i, k)
            else:
                for k in range(3):
                    work(lo, k)

        @block.sync
        def _(sp):
            with nc.allow_non_contiguous_dma(reason="small transposed vectors"):
                sp.dma_start(cT[:], cvec.rearrange("b d -> d b")).then_inc(ld_mod, 16)
                sp.dma_start(wcol[:, 0:1], ipw.partition_broadcast(128)).then_inc(ld_mod, 16)
                sp.dma_start(x_sb[:, :, cols(0)], x[0].rearrange("(m c) d -> m c d", c=C)).then_inc(ld_x[0], 16)
                sp.dma_start(wm[:], wmod).then_inc(ld_mod, 16)
                sp.dma_start(x_sb[:, :, cols(1)], x[1].rearrange("(m c) d -> m c d", c=C)).then_inc(ld_x[1], 16)
                sp.dma_start(rw[:], router_w).then_inc(ld_ffn, 16)
                sp.dma_start(rb[:], router_b.partition_broadcast(128)).then_inc(ld_ffn, 16)
                sp.dma_start(b2c[:, 0:1], sb2.rearrange("(h o) -> h o", o=1)).then_inc(ld_ffn, 16)
                sp.dma_start(b2r[:], eb2).then_inc(ld_ffn, 16)
                sp.dma_start(ws1[:], sw1).then_inc(ld_ffn, 16)
                sp.dma_start(ws2[:], sw2).then_inc(ld_ffn, 16)
                sp.dma_start(bs1[:], sb1.rearrange("(h o) -> h o", o=1)).then_inc(ld_ffn, 16)

            def write_shift():
                sp.dma_start(shift_d.rearrange("p (b h) (c m) -> p b (h c) m", b=B, c=C).rearrange("p b q m -> q p b m"),
                             spart[:].rearrange("q p (b m) -> q p b m", b=B)).then_inc(shift_wr, 16)

            def write_parts(b):
                for p in range(PARTS):
                    sp.wait_ge(cut_v, 8 * b + (5, 6, 8)[p])
                    sp.wait_ge(cut_a, 4 * b + (3, 4, 4)[p])
                    sp.dma_start(part_d[b * H:(b + 1) * H, p],
                                 part[:, b, p].rearrange("f s t -> f (s t)")).then_inc(part_wr[b], 16)

            def load_keys(dst, g, n, signal):
                for a in range(PARTS):
                    for r in range(PARTS):
                        at = HD * (PARTS * a + r)
                        sp.dma_start(dst[at:at + HD, 0:n], part_d[bass.ds(g, n), a, :, 0].rearrange("g d t -> d g t")
                                     ).then_inc(signal, 16)

            def load_queries(dst, g, n, signal):
                src = part_d[bass.ds(g, n)].rearrange("g p d s t -> (p d) g (s t)")
                for r in range(PARTS):
                    at = PARTS * HD * r
                    sp.dma_start(dst[at:at + PARTS * HD, 0:n].rearrange("k g s t -> k g (s t)"), src
                                 ).then_inc(signal, 16)

            def load_group(it, j):
                g = 2 * G * it + G * j
                for s in range(2):
                    sp.dma_start(qry[j][ROWS:KROWS, :, s], shift_d[:, bass.ds(g, G)]).then_inc(opnd[j], 16)
                load_keys(keys[j], g, G, opnd[j])
                load_queries(qry[j], g, G, opnd[j])

            sp.wait_ge(spart_ok, 1)
            write_shift()
            write_parts(0)
            exact = exact_wanted(sp)
            with sp.If(exact > 0):
                sp.wait_ge(part_wr[0], 16 * PARTS)
                sp.wait_ge(part_wr[1], 16 * PARTS)
                with sp.Fori(0, HG) as g:
                    sp.wait_ge(ex_max, C * g + C)
                    load_keys(keys[0], g, 1, ex_ld)
                    load_queries(qry[0], g, 1, ex_ld)
                sp.wait_ge(ex_max, C * HG + C)
                sp.wait_ge(shift_wr, 16)
                sp.wait_ge(spart_ok, 2)
                write_shift()
                sp.wait_ge(shift_wr, 32)

            sp.wait_ge(consts, 5)
            sp.wait_ge(shift_wr, 16)
            sp.wait_ge(part_wr[0], 16 * PARTS)
            for j in range(2):
                load_group(0, j)
            for k in range(3):
                sp.dma_start(w1[k][:], ew1[k]).then_inc(w_ld[k], 16)
                sp.dma_start(w2[k][:], ew2[k]).then_inc(w_ld[k], 16)
                sp.dma_start(b1[k][:], eb1[k].rearrange("(h o) -> h o", o=1)).then_inc(w_ld[k], 16)
            sp.wait_ge(part_wr[1], 16 * PARTS)
            with sp.Fori(1, ITERS) as it:
                for j in range(2):
                    sp.wait_ge(filled, BODY * it + SEC * (j + 1) - 1 - BODY)
                    load_group(it, j)

            def load_row(b, e, k):
                sp.dma_start(cwr[k], cw_d[b, bass.ds(e, 1), :]).then_inc(row_ld[k], 16)

            def load_weights(e, k):
                sp.dma_start(w1[k][:], ew1[e]).then_inc(w_ld[k], 16)
                sp.dma_start(w2[k][:], ew2[e]).then_inc(w_ld[k], 16)
                sp.dma_start(b1[k][:], eb1[e].rearrange("(h o) -> h o", o=1)).then_inc(w_ld[k], 16)

            for b in range(B):
                if b:
                    for k in range(3):
                        sp.wait_ge(l2_done, RING + chunk(0, E - 2 + k, FCH - 1) + 1)
                        load_weights(k, k)
                sp.wait_ge(cwT_ok, b + 1)
                sp.dma_start(cw_d[b], cwT[:, b]).then_inc(cw_wr, 16)
                sp.wait_ge(cw_wr, 16 * b + 16)
                for k in range(3):
                    if b:
                        sp.wait_ge(cwb_ok, E - 2 + k)
                    load_row(b, k, k)
                with sp.Fori(1, E // 3) as i:
                    for k in range(3):
                        sp.wait_ge(cwb_ok, E * b + 3 * i + k - 2)
                        load_row(b, 3 * i + k, k)
                        sp.wait_ge(l2_done, RING + chunk(b, 3 * i + k - 2, FCH - 1) + 1)
                        load_weights(3 * i + k, k)

            out_v = out.rearrange("b (m c) d -> b m c d", c=C)
            for b in range(B):
                sp.wait_ge(y_ok, b + 1)
                sp.dma_start(out_v[b], h_sb[:, :, cols(b)]).then_inc(out_wr, 16)
            sp.wait_ge(out_wr, 16 * B)

        @block.gpsimd
        def _(pool):
            pool.sem_inc(gat_ok, RING)
            nc.gpsimd.memset(ones[:], 1.0).then_inc(consts, 1)
            nc.gpsimd.memset(ident[:], 0.0).then_inc(pool_seq, 1)
            pool.wait_ge(pool_seq, 1)
            nc.gpsimd.affine_select(out=ident[:], in_=ident[:], compare_op=ALU.not_equal, fill=1.0, base=0,
                                    pattern=[[-1, 128]], channel_multiplier=1).then_inc(consts, 1)
            nc.gpsimd.iota(iota[:], [[1, E]], base=0, channel_multiplier=0,
                           allow_small_or_imprecise_dtypes=True).then_inc(consts, 1)
            for j in range(2):
                nc.gpsimd.memset(val[j][:], 0.0).then_inc(pool_seq, 1)
            pool.wait_ge(pool_seq, 3)
            for j in range(2):
                last = nc.gpsimd.memset(val[j][:, :, :, HD:HD + 1], 1.0)
            last.then_inc(consts, 1)
            for j in range(2):
                last = nc.gpsimd.memset(keys[j][:], 1.0)
            last.then_inc(consts, 1)

            def copy_values(it, j):
                at = 2 * G * HD * it + G * HD * j
                nc.gpsimd.tensor_copy(val[j][:, :, :, 0:HD],
                                      h_sb[:, :, bass.ds(at, G * HD)].rearrange("m c (q d) -> m c q d", q=G)
                                      ).then_inc(val_ok[j], 1)

            pool.wait_ge(h_ok, 1)
            pool.wait_ge(consts, 5)
            for j in range(2):
                copy_values(0, j)
            for p in range(PARTS):
                pool.wait_ge(cut_v, 8 + (5, 6, 8)[p])
                pool.wait_ge(cut_a, 4 + (3, 4, 4)[p])
                pool.dma_start(part_d[H:2 * H, p], part[:, 1, p].rearrange("f s t -> f (s t)")).then_inc(part_wr[1], 16)
            pool.wait_ge(h_ok, 2)
            with pool.Fori(1, ITERS) as it:
                for j in range(2):
                    pool.wait_ge(pv_done, pv_count(it, -C if j == 0 else 0, HALVES - 1))
                    copy_values(it, j)

            def spread(b, i, k):
                pool.wait_ge(row_ld[k], 16 * (E // 3 * b + i + 1))
                pool.wait_ge(pool_seq, 3 + E * b + 3 * i + k)
                nc.gpsimd.tensor_tensor(spare[:], ones[0:1, 0:1], ones[0:1, 0:1], ALU.mult).then_inc(pool_seq, 1)
                nc.gpsimd.partition_broadcast(cwb[k], cwr[k], 128).then_inc(cwb_ok, 1)

            for q in range(FCH):
                pool.wait_ge(hid_ok, UPB + q + 1)
                nc.gpsimd.tensor_copy(gat[:, q + 4], hid[:, q + 4]).then_inc(gat_ok, 1)

            def weight(i, k):
                spread(0, i, k)
                for q in range(FCH):
                    n = chunk(0, 3 * i + k + 1, q)
                    pool.wait_ge(cwb_ok, 3 * i + k + 1)
                    pool.wait_ge(hid_ok, UPB + n + 1)
                    pool.wait_ge(l2_done, n + 1)
                    nc.gpsimd.tensor_tensor(gat[:, 2 * k + q], hid[:, 2 * k + q], cwb[k][:, q * CH:(q + 1) * CH],
                                            ALU.mult).then_inc(gat_ok, 1)

            experts(pool, 0, 0, E // 3, weight)

            def spread1(i, k):
                pool.wait_ge(gat_ok, RING + chunk(1, 3 * i + k - 1, 0))
                spread(1, i, k)

            experts(pool, 1, 0, E // 3, spread1)

        @block.scalar
        def _(act):
            seq = [0]

            def link(ins):
                seq[0] += 1
                ins.then_inc(act_seq, 1)
                act.wait_ge(act_seq, seq[0])

            act.sem_inc(hid_ok, UPB)
            act.wait_ge(ld_mod, 48)
            nc.scalar.activation(sil[:, 0], cT[:], ACT.Exp, scale=-1.0).then_inc(act_exp, 1)
            nc.scalar.activation(wcol[:, 1:2], wcol[:, 0:1], ACT.Exp, scale=-1.0).then_inc(act_exp, 1)

            act.wait_ge(silu_ok, 3)
            for b in range(B):
                if b:
                    act.wait_ge(cut_v, 8 * b)
                for half in range(HALVES):
                    act.wait_ge(hT_mm, HALVES * b + half + 1)
                    at = slice(half * CH, (half + 1) * CH)
                    nc.scalar.activation(hT[:, b * T + half * CH:b * T + (half + 1) * CH], slot[b][:, at],
                                         ACT.Copy).then_inc(hT_ok, 1)
                    link(nc.scalar.activation(hw[:, at], slot[b][:, at], ACT.Copy, scale=wcol[:, 2:3]))
                    nc.scalar.activation(part[:, b, 0, 1, at], hw[:, at], ACT.Copy).then_inc(cut_a, 1)
                    act.wait_ge(rem_ok, HALVES * b + half + 1)
                    nc.scalar.activation(part[:, b, 1, 1, at], rem[:, 1, at], ACT.Copy).then_inc(cut_a, 1)

            def h2_to_sbuf(b, src):
                nc.scalar.activation(hT[:, b * T:(b + 1) * T], src[:], ACT.Copy).then_inc(h2T_ok, 1)

            def exp_logits(b):
                act.wait_ge(lsub, b + 1)
                nc.scalar.activation(lg[:, b, 1], lg[:, b, 0], ACT.Exp).then_inc(lexp, 1)

            def weights_to_sbuf(b, src):
                nc.scalar.activation(cwT[:, b], src[0:E, :], ACT.Copy).then_inc(cwT_ok, 1)

            def exps(it, body):
                for r, (kind, j, c, q) in enumerate(body):
                    if kind in ("none", "turn", "logit"):
                        continue
                    act.wait_ge(filled, fill_count(it, r, body))
                    if kind == "h2T":
                        h2_to_sbuf(0, slot[r % SLOTS])
                    elif kind == "cwT":
                        weights_to_sbuf(0, slot[r % SLOTS])
                    else:
                        step = C * j + c
                        if q == 0 and not (body is FIRST and step < 2):
                            act.wait_ge(pv_done, pv_count(it, step - 1, HALVES - 1))
                        nc.scalar.activation(prob[c % 2][:, q, :], slot[r % SLOTS][:], ACT.Exp,
                                             scale=SCALE).then_inc(exp_done, 1)
                    if body is LAST and r == LOGIT_AT + 4:
                        exp_logits(0)

            exps(0, FIRST)
            with act.Fori(1, ITERS - 1) as it:
                exps(it, MIDDLE)
            exps(ITERS - 1, LAST)

            def hidden(b, m, at, bias, after=None):
                for q in range(FCH):
                    n = chunk(b, m, q)
                    act.wait_ge(l1_done, n + 1)
                    act.wait_ge(gat_ok, RING + n - q if after else n + 1)
                    nc.scalar.activation(hid[:, at + q], up_bank[(at + q) % UPB], ACT.Relu,
                                         bias=bias).then_inc(hid_ok, 1)

            def gated(b):
                act.wait_ge(ffn_mm, b + 1)
                for q in range(FCH):
                    nc.scalar.activation(hT[:, b * T + q * CH:b * T + (q + 1) * CH], acc[:, q * CH:(q + 1) * CH],
                                         ACT.Identity, bias=gbT[:, 3, b:b + 1], scale=gbT[:, 2, b:b + 1]
                                         ).then_inc(ffT_ok, 1)

            hidden(0, 0, 4, bs1[:])

            def routed0(i, k):
                hidden(0, 3 * i + k + 1, 2 * k, b1[k][:])

            experts(act, 0, 0, 2, routed0)
            act.wait_ge(h2T_mm, 1)
            h2_to_sbuf(1, slot[2])
            experts(act, 0, 2, 3, routed0)
            routed0(3, 0)
            exp_logits(1)
            routed0(3, 1)
            routed0(3, 2)
            act.wait_ge(cwT_mm, 1)
            weights_to_sbuf(1, slot[2])
            experts(act, 0, 4, 5, routed0)
            gated(0)
            hidden(1, 0, 4, bs1[:], after=True)
            experts(act, 1, 0, E // 3, lambda i, k: hidden(1, 3 * i + k + 1, 2 * k, b1[k][:]))
            gated(1)

        @block.vector
        def _(dve):
            seq = [0]
            v = nc.vector

            def link(ins):
                seq[0] += 1
                ins.then_inc(dve_seq, 1)
                dve.wait_ge(dve_seq, seq[0])

            dve.wait_ge(act_exp, 2)
            link(v.tensor_scalar(sil[:, 1], sil[:, 0], 1.0, None, ALU.add))
            link(v.reciprocal(sil[:, 2], sil[:, 1]))
            link(v.tensor_tensor(sil[:, 3], sil[:, 2], cT[:], ALU.mult))
            dve.wait_ge(consts, 2)
            for b in range(B):
                v.tensor_scalar(silb[:, b], ones[:], sil[:, 3, b:b + 1], None, ALU.mult).then_inc(silu_ok, 1)
            link(v.tensor_scalar(wcol[:, 1:2], wcol[:, 1:2], 1.0, None, ALU.add))
            v.reciprocal(wcol[:, 2:3], wcol[:, 1:2]).then_inc(silu_ok, 1)

            def statistics(src, b):
                for c in range(C):
                    last = v.bn_stats(stats[:, c], src[:, c, cols(b)])
                link(last)
                for c in range(C):
                    last = v.bn_aggr(mv[:, b, c], stats[:, c])
                link(last)
                var, y, t = rstd[:, b, 0], rstd[:, b, 1], rstd[:, b, 2]
                link(v.tensor_scalar(var, mv[:, b, :, 1], EPS, None, ALU.add))
                link(v.tensor_scalar(rint[:, b, 0], var.bitcast(I32), 1, None, ALU.logical_shift_right))
                link(v.tensor_scalar(rint[:, b, 1], rint[:, b, 0], -1.0, float(0x5F3759DF), ALU.mult, ALU.add))
                link(v.tensor_copy(y, rint[:, b, 1].bitcast(F32)))
                for _ in range(3):
                    link(v.tensor_tensor(t, y, y, ALU.mult))
                    link(v.scalar_tensor_tensor(t, t, -0.5, var, ALU.mult, ALU.mult))
                    link(v.scalar_tensor_tensor(y, t, 1.5, y, ALU.add, ALU.mult))

            def over_classes(row):
                return row.unsqueeze(1).broadcast_to((128, C, D))

            def normalised(src, b, add_row, mul_row):
                for c in range(C):
                    last = v.tensor_scalar(h_sb[:, c, cols(b)], src[:, c, cols(b)], mv[:, b, c, 0:1],
                                           rstd[:, b, 1, c:c + 1], ALU.subtract, ALU.mult)
                link(last)
                h_b = h_sb[:, :, cols(b)]
                link(v.tensor_tensor(h_b, h_b, over_classes(mod[:, mul_row, cols(b)]), ALU.mult))
                return v.tensor_tensor(h_b, h_b, over_classes(mod[:, add_row, cols(b)]), ALU.add)

            def take_modulation(ks):
                for b in range(B):
                    for k in ks:
                        src = (acc, slot[2])[b][:, k * D:(k + 1) * D]
                        if k in (1, 4):
                            last = v.tensor_scalar(mod[:, k, cols(b)], src, 1.0, None, ALU.add)
                        else:
                            last = v.tensor_copy(mod[:, k, cols(b)], src)
                return last

            def gate(dst, tmp):
                link(v.tensor_scalar(tmp, dst, -1.0, 0.25, ALU.mult, ALU.max))
                link(v.tensor_tensor(tmp, tmp, dst, ALU.max))
                link(v.tensor_scalar(dst, dst, 0.0, 2.0, ALU.is_ge, ALU.mult))
                link(v.scalar_tensor_tensor(dst, dst, -1.0, tmp, ALU.add, ALU.mult))

            def cut(b):
                for half in range(HALVES):
                    at = slice(half * CH, (half + 1) * CH)
                    src = hT[:, b * T + half * CH:b * T + (half + 1) * CH]
                    n = HALVES * b + half
                    dve.wait_ge(hT_ok, n + 1)
                    v.tensor_copy(part[:, b, 0, 0, at], src).then_inc(cut_v, 1)
                    dve.wait_ge(cut_a, 2 * n + 1)
                    v.tensor_tensor(rem[:, 1, at], hw[:, at], part[:, b, 0, 1, at], ALU.subtract).then_inc(rem_ok, 1)
                    dve.wait_ge(cut_v, 4 * n + 1)
                    link(v.tensor_tensor(rem[:, 0, at], src, part[:, b, 0, 0, at], ALU.subtract))
                    v.tensor_copy(part[:, b, 1, 0, at], rem[:, 0, at]).then_inc(cut_v, 1)
                    dve.wait_ge(cut_v, 4 * n + 2)
                    v.tensor_tensor(part[:, b, 2, 0, at], rem[:, 0, at], part[:, b, 1, 0, at],
                                    ALU.subtract).then_inc(cut_v, 1)
                    dve.wait_ge(cut_a, 2 * n + 2)
                    v.tensor_tensor(part[:, b, 2, 1, at], rem[:, 1, at], part[:, b, 1, 1, at],
                                    ALU.subtract).then_inc(cut_v, 1)

            dve.wait_ge(ld_x[0], 16)
            statistics(x_sb, 0)
            dve.wait_ge(mod_mm, 1)
            link(take_modulation((0, 1)))
            normalised(x_sb, 0, 0, 1).then_inc(h_ok, 1)

            link(v.tensor_reduce(reach[:, 0:1], mod[:, 1], AX.X, ALU.max, apply_absolute_value=True))
            link(v.tensor_reduce(reach[:, 1:2], mod[:, 0], AX.X, ALU.max, apply_absolute_value=True))
            link(v.tensor_scalar(reach[:, 2:3], reach[:, 1:2], float(HD) ** 0.5, None, ALU.mult))
            link(v.scalar_tensor_tensor(reach[:, 3:4], reach[:, 0:1], float(D) ** 0.5, reach[:, 2:3], ALU.mult, ALU.add))
            link(v.scalar_tensor_tensor(reach[:, 4:5], reach[:, 3:4], -ROUNDING, reach[:, 3:4], ALU.mult, ALU.mult))
            limit = 1.0 if force_exact else -SAFE_EXPONENT / SCALE
            v.tensor_scalar(flag[:], reach[:, 4:5], limit, None, ALU.is_lt).then_inc(flag_ok, 1)
            link(v.tensor_copy(spart1[:, 0:1], reach[:, 4:5]))
            link(v.tensor_tensor(reach[:, 5:6], reach[:, 4:5], spart1[:, 0:1], ALU.subtract))
            link(v.tensor_copy(spart1[:, 1:2], reach[:, 5:6]))
            link(v.tensor_tensor(spart1[:, 2:3], reach[:, 5:6], spart1[:, 1:2], ALU.subtract))
            v.tensor_copy(spart[:], spart1[:].unsqueeze(2).broadcast_to((128, PARTS, B * 128))).then_inc(spart_ok, 1)

            dve.wait_ge(ld_x[1], 16)
            cut(0)
            statistics(x_sb, 1)
            normalised(x_sb, 1, 0, 1).then_inc(h_ok, 1)
            link(take_modulation((2, 3, 4)))
            v.tensor_copy(gbT[:, 0], acc[:, T - B:T]).then_inc(mod_used, 1)
            cut(1)

            exact = exact_wanted(dve)
            with dve.If(exact > 0):
                dve.sem_inc(ex_max, C)
                with dve.Fori(0, HG) as g:
                    for c in range(C):
                        dve.wait_ge(ex_mm, C * g + c + 1)
                        v.reduce_max(shift[:].rearrange("p g c -> p (g c)")[:, bass.ds(C * g + c, 1)],
                                     slot[c % 2][:], AX.X, negate=True).then_inc(ex_max, 1)
                dve.wait_ge(shiftT_mm, 1)
                dve.wait_ge(shift_wr, 16)
                sT = acc[:, 0:B * 128]
                v.tensor_copy(spart[:, 0], sT).then_inc(ex_seq, 1)
                dve.wait_ge(ex_seq, 1)
                v.tensor_tensor(srem[:], sT, spart[:, 0], ALU.subtract).then_inc(ex_seq, 1)
                dve.wait_ge(ex_seq, 2)
                v.tensor_copy(spart[:, 1], srem[:]).then_inc(ex_seq, 1)
                dve.wait_ge(ex_seq, 3)
                v.tensor_tensor(spart[:, 2], srem[:], spart[:, 1], ALU.subtract).then_inc(spart_ok, 1)

            dve.wait_ge(mod_used, 1)
            gate(mod[:, 2], modt[:])
            gate(gbT[:, 0], gbT[:, 1])
            dve.wait_ge(ld_ffn, 112)
            link(v.tensor_copy(gbT[:, 2], gbT[:, 0]))
            link(v.tensor_scalar(gbT[:, 3], gbT[:, 0], b2c[:, 0:1], None, ALU.mult))

            def take_sums(it, j):
                for half in range(HALVES):
                    dve.wait_ge(pv_done, pv_count(it, C * j, half))
                    v.tensor_copy(oT[:, half * CH:(half + 1) * CH],
                                  acc[:, half * CH:(half + 1) * CH]).then_inc(evac, 1)

            def divide(it, j, count, src):
                dve.wait_ge(filled, count)
                sums = src[:].rearrange("m (c q k) -> m c q k", c=C, q=G)
                link(v.reciprocal(rden[:], sums[:, :, :, HD]))
                at = G * HD * (2 * it + j - 1)
                v.tensor_tensor(attn[:, :, at:at + G * HD].rearrange("m c (q d) -> m c q d", q=G),
                                sums[:, :, :, 0:HD], rden[:].unsqueeze(3).broadcast_to((128, C, G, HD)),
                                ALU.mult).then_inc(norm_done, 1)

            def residual(b):
                a = attn[:, :, cols(b)]
                link(v.tensor_tensor(a, a, over_classes(mod[:, 2, cols(b)]), ALU.mult))
                link(v.tensor_tensor(a, a, x_sb[:, :, cols(b)], ALU.add))

            def route(b, src):
                def over_tiles(row):
                    return row.unsqueeze(1).broadcast_to((128, C, E))

                def over_experts(col):
                    return col.unsqueeze(2).broadcast_to((128, C, E))

                l0, l1, l2, l3 = (lg[:, b, k] for k in range(4))
                link(v.tensor_tensor(l0, src[:, 0:16 * C].rearrange("p (t e) -> p t e", e=16)[:, :, 0:E],
                                     over_tiles(rb[:]), ALU.add))
                link(v.reduce_max(lred[:, b, 0], l0, AX.X))
                v.tensor_tensor(l0, l0, over_experts(lred[:, b, 0]), ALU.subtract).then_inc(lsub, 1)
                dve.wait_ge(lexp, b + 1)
                link(v.tensor_reduce(lred[:, b, 1], l1, AX.X, ALU.add))
                link(v.reciprocal(lred[:, b, 2], lred[:, b, 1]))
                link(v.tensor_tensor(l0, l1, over_experts(lred[:, b, 2]), ALU.mult))
                for c in range(C):
                    last = v.max(top[:, b, c], l0[:, c])
                link(last)
                for c in range(C):
                    last = v.max_index(topi[:, b, c], top[:, b, c], l0[:, c])
                link(last)
                link(v.tensor_copy(topf[:, b], topi[:, b]))
                link(v.tensor_tensor(l1, over_tiles(iota[:]), over_experts(topf[:, b, :, 0]), ALU.is_equal))
                for k in range(1, K):
                    link(v.tensor_tensor(l2, over_tiles(iota[:]), over_experts(topf[:, b, :, k]), ALU.is_equal))
                    link(v.tensor_tensor(l1, l1, l2, ALU.add))
                v.tensor_tensor(l3, l0, l1, ALU.mult).then_inc(cw_ok, 1)

            for it in range(ITERS):
                body = FIRST if it == 0 else LAST if it == ITERS - 1 else MIDDLE
                for j in range(2):
                    if it + j == 0:
                        continue
                    take_sums(it, j)
                    r = body.index(("turn", j, 0, 0))
                    divide(it, j, fill_count(it, r, body), slot[r % SLOTS])
                    if (it, j) == (ITERS // 2, 0):
                        dve.wait_ge(norm_done, norm_count(it, j))
                        residual(0)
                        statistics(attn, 0)
                        normalised(attn, 0, 3, 4).then_inc(h_ok, 1)
                    if (it, j) == (ITERS - 1, 0):
                        r = body.index(("logit", 0, 0, 0))
                        dve.wait_ge(filled, fill_count(it, r, body))
                        route(0, slot[r % SLOTS])
            take_sums(ITERS, 0)
            divide(ITERS, 0, fill_count(ITERS - 1, len(LAST), LAST) + 1, slot[2])
            dve.wait_ge(norm_done, norm_count(ITERS, 0))
            residual(1)
            statistics(attn, 1)
            normalised(attn, 1, 3, 4).then_inc(h_ok, 1)
            dve.wait_ge(logit_mm, 1)
            route(1, slot[2])

            for q in range(FCH):
                dve.wait_ge(hid_ok, UPB + chunk(1, 0, q) + 1)
                dve.wait_ge(l2_done, RING + FALL)
                v.tensor_copy(gat[:, q + 4], hid[:, q + 4]).then_inc(gat_ok, 1)

            def weight(i, k):
                dve.wait_ge(cwb_ok, E + 3 * i + k + 1)
                for q in range(FCH):
                    n = chunk(1, 3 * i + k + 1, q)
                    dve.wait_ge(hid_ok, UPB + n + 1)
                    dve.wait_ge(l2_done, n + 1)
                    v.tensor_tensor(gat[:, 2 * k + q], hid[:, 2 * k + q], cwb[k][:, q * CH:(q + 1) * CH],
                                    ALU.mult).then_inc(gat_ok, 1)

            experts(dve, 1, 0, E // 3, weight)

            for b in range(B):
                dve.wait_ge(y_mm, b + 1)
                v.tensor_tensor(h_sb[:, :, cols(b)], attn[:, :, cols(b)],
                                slot[b][:].rearrange("m (c d) -> m c d", c=C), ALU.add).then_inc(y_ok, 1)

        @block.tensor
        def _(pe):
            mm = nc.tensor.matmul

            def turn(dst, src, lo=0, hi=C):
                for c in range(lo, hi):
                    last = nc.tensor.transpose(dst[:, c * M:(c + 1) * M], src(c), ident[:])
                return last

            pe.sem_inc(l2_done, RING)
            pe.wait_ge(ld_mod, 48)
            pe.wait_ge(silu_ok, 2)
            for b, dst in enumerate((acc, slot[2])):
                mm(dst[:, 0:CH], silb[:, b], wm[:, 0:CH], start=True, stop=True)
                mm(dst[:, CH:5 * D], silb[:, b], wm[:, CH:5 * D], start=True, stop=True)
            mm(acc[:, T - B:T], wm[:, 5 * D:6 * D], sil[:, 3], start=True, stop=True).then_inc(mod_mm, 1)
            pe.wait_ge(consts, 2)
            for b in range(B):
                pe.wait_ge(h_ok, b + 1)
                for half in range(HALVES):
                    turn(slot[b], lambda c: h_sb[:, c, cols(b)], half * C // HALVES,
                         (half + 1) * C // HALVES).then_inc(hT_mm, 1)

            def scores(dst, j, q, c, rows):
                k_c = keys[j][0:rows, q, c * M:(c + 1) * M]
                for half in range(HALVES):
                    lo, hi = half * CH, (half + 1) * CH
                    cuts = [(lo, hi, 1)]
                    if lo <= c * M < hi:
                        cuts = [(lo, c * M, 1), (c * M, (c + 1) * M, 0), ((c + 1) * M, hi, 1)]
                    for a, z, s in cuts:
                        if z > a:
                            last = mm(dst[:, a:z], k_c, qry[j][0:rows, q, s, a:z], start=True, stop=True)
                return last

            exact = exact_wanted(pe)
            with pe.If(exact > 0):
                pe.wait_ge(cut_a, 4 * B)
                with pe.Fori(0, HG) as g:
                    pe.wait_ge(ex_ld, 16 * (KEY_LOADS + QUERY_LOADS) * (g + 1))
                    for c in range(C):
                        pe.wait_ge(ex_max, C * g + c + C - 1)
                        scores(slot[c % 2], 0, 0, c, ROWS).then_inc(ex_mm, 1)
                pe.wait_ge(ex_max, C * HG + C)
                pe.wait_ge(mod_used, 1)
                for b in range(B):
                    last = nc.tensor.transpose(acc[:, b * 128:(b + 1) * 128],
                                               shift[:, b * H:(b + 1) * H].rearrange("p h c -> p (h c)"), ident[:])
                last.then_inc(shiftT_mm, 1)
                pe.wait_ge(spart_ok, 2)

            def weigh(jv, cp, half):
                for q in range(G):
                    last = mm(acc[32 * q:32 * q + 32, half * CH:(half + 1) * CH], val[jv][:, cp, q, :],
                              prob[cp % 2][:, q, half * CH:(half + 1) * CH], start=cp == 0, stop=cp == C - 1,
                              tile_position=(0, 32 * q))
                last.then_inc(pv_done, 1)

            def logits(b, dst):
                for c in range(C):
                    last = mm(dst[:, 16 * c:16 * c + E], hT[:, b * T + c * M:b * T + (c + 1) * M], rw[:],
                              start=True, stop=True)
                return last

            def turn_weights(b, dst):
                return turn(dst[0:E], lambda c: lg[:, b, 3, c])

            def free_slot(it, r, body):
                p = r - SLOTS
                while p >= 0 and body[p][0] == "none":
                    p -= SLOTS
                if p < 0:
                    if body is not FIRST:
                        pe.wait_ge(exp_done, exp_count(it, p + 1))
                    return
                kind, j = body[p][0:2]
                if kind == "turn":
                    pe.wait_ge(norm_done, norm_count(it, j))
                elif kind == "h2T":
                    pe.wait_ge(h2T_ok, 1)
                elif kind == "logit":
                    pe.wait_ge(lsub, 1)
                elif kind == "cwT":
                    pe.wait_ge(cwT_ok, 1)
                else:
                    pe.wait_ge(exp_done, exp_count(it, sum(u[0] == "score" for u in body[:p + 1])))

            def attend(it, body):
                for r, (kind, j, c, q) in enumerate(body):
                    if kind == "none":
                        continue
                    dst = slot[r % SLOTS]
                    free_slot(it, r, body)
                    if kind == "turn":
                        pe.wait_ge(evac, evac_count(it, j, HALVES - 1))
                        turn(dst, lambda c: oT[:, c * M:(c + 1) * M]).then_inc(filled, 1)
                    elif kind == "h2T":
                        pe.wait_ge(h_ok, 3)
                        turn(dst, lambda c: h_sb[:, c, cols(0)]).then_inc(filled, 1)
                    elif kind == "logit":
                        pe.wait_ge(h2T_ok, 1)
                        pe.wait_ge(ld_ffn, 112)
                        logits(0, dst).then_inc(filled, 1)
                    elif kind == "cwT":
                        pe.wait_ge(cw_ok, 1)
                        turn_weights(0, dst).then_inc(filled, 1)
                    if kind != "score":
                        continue
                    if c == 0 and q == 0:
                        pe.wait_ge(opnd[j], 16 * (KEY_LOADS + QUERY_LOADS + SHIFT_LOADS) * (it + 1))
                    scores(dst, j, q, c, KROWS).then_inc(filled, 1)
                    step = C * j + c
                    if q % 2 == 1 and not (body is FIRST and step == 0):
                        half, cp, jp = q // 2, (c - 1) % C, j if c else 1 - j
                        if half == 0:
                            pe.wait_ge(exp_done, exp_count(it, G * step))
                            if cp == 0:
                                pe.wait_ge(val_ok[jp], it + 1)
                        if cp == 0 and not (body is FIRST and j == 0):
                            pe.wait_ge(evac, evac_count(it, j, half))
                        weigh(jp, cp, half)

            pe.wait_ge(mod_used, 1)
            pe.wait_ge(cut_a, 4 * B)
            attend(0, FIRST)
            with pe.Fori(1, ITERS - 1) as it:
                attend(it, MIDDLE)
            attend(ITERS - 1, LAST)
            pe.wait_ge(exp_done, exp_count(ITERS, 0))
            for half in range(HALVES):
                weigh(1, C - 1, half)

            def up(b, m, at, w, fresh=False):
                for q in range(FCH):
                    n = chunk(b, m, q)
                    pe.wait_ge(hid_ok, UPB + n - q if fresh else n + 1)
                    mm(up_bank[(at + q) % UPB], w[:], hT[:, b * T + q * CH:b * T + (q + 1) * CH],
                       start=True, stop=True).then_inc(l1_done, 1)

            def down(b, m, at, w, start=False):
                for q in range(FCH):
                    pe.wait_ge(gat_ok, RING + chunk(b, m, q) + 1)
                    mm(acc[:, q * CH:(q + 1) * CH], w[:], gat[:, at + q], start=start, stop=False).then_inc(l2_done, 1)

            def loaded(b, i, k):
                pe.wait_ge(w_ld[k], 48 * (E // 3 * b + i + 1))

            def routed(b, i, k, last=False):
                if not last:
                    k1, i1 = (k + 1) % 3, i + (k + 1) // 3
                    loaded(b, i1, k1)
                    up(b, 3 * i + k + 2, 2 * k1, w1[k1])
                down(b, 3 * i + k + 1, 2 * k, w2[k])

            def close(b):
                for q in range(FCH):
                    last = mm(acc[:, q * CH:(q + 1) * CH], b2r[:], cwT[:, b, q * CH:(q + 1) * CH], start=False, stop=True)
                last.then_inc(ffn_mm, 1)

            pe.wait_ge(h2T_ok, 1)
            pe.wait_ge(ld_ffn, 112)
            up(0, 0, 4, ws1)
            pe.wait_ge(evac, evac_count(ITERS, 0, HALVES - 1))
            turn(slot[2], lambda c: oT[:, c * M:(c + 1) * M]).then_inc(filled, 1)
            loaded(0, 0, 0)
            up(0, 1, 0, w1[0])
            down(0, 0, 4, ws2, start=True)
            experts(pe, 0, 0, 2, lambda i, k: routed(0, i, k))
            pe.wait_ge(h_ok, 4)
            turn(slot[2], lambda c: h_sb[:, c, cols(1)]).then_inc(h2T_mm, 1)
            experts(pe, 0, 2, 3, lambda i, k: routed(0, i, k))
            pe.wait_ge(h2T_ok, 2)
            logits(1, slot[2]).then_inc(logit_mm, 1)
            experts(pe, 0, 3, 4, lambda i, k: routed(0, i, k))
            pe.wait_ge(cw_ok, 2)
            turn_weights(1, slot[2]).then_inc(cwT_mm, 1)
            experts(pe, 0, 4, 5, lambda i, k: routed(0, i, k, last=k == 2))
            close(0)

            up(1, 0, 4, ws1, fresh=True)
            loaded(1, 0, 0)
            up(1, 1, 0, w1[0])
            pe.wait_ge(ffT_ok, FCH)
            down(1, 0, 4, ws2, start=True)
            experts(pe, 1, 0, E // 3 - 1, lambda i, k: routed(1, i, k))
            experts(pe, 1, E // 3 - 1, E // 3, lambda i, k: routed(1, i, k, last=k == 2))
            pe.wait_ge(cwT_ok, 2)
            close(1)
            pe.wait_ge(hid_ok, UPB + 2 * FALL)
            for b in range(B):
                pe.wait_ge(ffT_ok, FCH * (b + 1))
                turn(slot[b], lambda c: hT[:, b * T + c * M:b * T + (c + 1) * M]).then_inc(y_mm, 1)


_INS = ["L0_attn_x", "L0_attn_inter_palace_weight", "L0_ffn_router_W", "L0_ffn_router_b", "L0_ffn_sW1",
        "L0_ffn_sb1", "L0_ffn_sW2", "L0_ffn_sb2", "L0_ffn_eW1", "L0_ffn_eb1", "L0_ffn_eW2", "L0_ffn_eb2",
        "L0_c", "L0_wmod"]


def kernel(**inputs):
    import numpy as np
    import concourse.bacc as bacc
    from concourse.bass_utils import run_bass_kernel_spmd

    nc = bacc.Bacc("TRN2", target_bir_lowering=False, num_devices=1)
    arrays, args = {}, []
    for name in _INS:
        a = np.ascontiguousarray(inputs[name])
        if a.ndim == 0:
            a = a.reshape(1)
        arrays[f"in_{name}"] = a
        args.append(nc.dram_tensor(f"in_{name}", a.shape, mybir.dt.from_np(a.dtype), kind="ExternalInput").ap())
    out = nc.dram_tensor("out", (B, T, D), F32, kind="ExternalOutput").ap()
    adaln_block(nc, *args, out)
    r = run_bass_kernel_spmd(nc, [arrays], core_ids=[0])
    return r.results[0]["out"]
```

```python
from contextlib import ExitStack

import concourse.bass as bass
from concourse import mybir

F32 = mybir.dt.float32
F32R = mybir.dt.float32r
BF16 = mybir.dt.bfloat16
I32 = mybir.dt.int32
U32 = mybir.dt.uint32
ALU = mybir.AluOpType
ACT = mybir.ActivationFunctionType
AX = mybir.AxisListType
RMAX = bass.bass_isa.ReduceOp.max

B, T, D = 2, 1024, 128
H, HD = 16, 8
C = 8
M = T // C
E, K = 15, 3
NT = B * T
TILES = B * C
HG = B * H
G = 4
EPS = 1e-5
SCALE = HD ** -0.5
SAFE_EXPONENT = 60.0
ROUNDING = 1.001
PARTS = 3
ROWS = PARTS * PARTS * HD
KROWS = ROWS + PARTS
NG = HG // G
KEY_LOADS, QUERY_LOADS, SHIFT_LOADS = PARTS, 1, 2
STEPS = 2 * C
ITERS = HG // G // 2
SEC = G * C + 1
BODY = 2 * SEC
OUT_AT = 6
H2T_AT, LOGIT_AT, CWT_AT = 12, 20, SEC + 18
SLOTS = 3
CH = 512
HALVES = T // CH
FCH = T // CH
FALL = FCH * (E + 1)
UPB = 3
WARM_UP = 10
RING = 6


def adaln_block(nc, x, ipw, router_w, router_b, sw1, sb1, sw2, sb2, ew1, eb1, ew2, eb2, cvec, wmod, out,
                force_exact=False):
    ctx = ExitStack()
    with ctx:
        def sb(name, shape, dt=F32):
            return ctx.enter_context(nc.sbuf_tensor(name, shape, dt))

        def ps(name, shape):
            return ctx.enter_context(nc.psum_tensor(name, shape, F32))

        def sem(name):
            return ctx.enter_context(nc.semaphore(name))

        x_sb = sb("x_sb", [128, C, B * D])
        h_sb = sb("h_sb", [128, C, B * D])
        attn = sb("attn", [128, C, B * D])
        hT = sb("hT", [128, NT])
        part = sb("part", [128, B, PARTS, 2, T], BF16)
        val = [sb(f"val{j}", [128, C, G, 32]) for j in range(2)]
        prob = [sb(f"prob{j}", [128, G, T]) for j in range(2)]
        oT = sb("oT", [128, T])
        rden = sb("rden", [128, C, G])
        ident = sb("ident", [128, 128])
        ones = sb("ones", [128, 128])
        cT = sb("cT", [128, B])
        sil = sb("sil", [128, 4, B])
        mod = sb("mod", [128, 5, B * D])
        modt = sb("modt", [128, B * D])
        gbT = sb("gbT", [128, 4, B])
        modT = sb("modT", [128, 3, B])
        aff = sb("aff", [128, 3, B])
        wcol = sb("wcol", [128, 3])
        stats = sb("stats", [128, B, C, 6])
        mv = sb("mv", [128, B, C, 2])
        rstd = sb("rstd", [128, B, 3, C])
        rint = sb("rint", [128, B, 2, C], I32)
        reach = sb("reach", [128, 8])
        flag = sb("flag", [128, 1], I32)
        shift = sb("shift", [128, HG, C])
        srem = sb("srem", [128, B * 128])
        spart1 = sb("spart1", [128, PARTS], BF16)
        spart = sb("spart", [128, PARTS, B * 128], BF16)
        rw = sb("rw", [128, E])
        rb = sb("rb", [128, E])
        b1 = [sb(f"b1_{k}", [128, 1]) for k in range(3)]
        b2c = sb("b2c", [128, 3])
        b2r = sb("b2r", [E, D])
        w1 = [sb(f"w1_{k}", [128, 2, D]) for k in range(3)]
        w1r = [sb(f"w1r_{k}", [128, 2, D], F32R) for k in range(3)]
        w2 = [sb(f"w2_{k}", [128, D]) for k in range(3)]
        iota = sb("iota", [128, E])
        lg = sb("lg", [128, B, 4, C, E])
        lred = sb("lred", [128, B, 3, C])
        top = sb("top", [128, B, C, 8])
        topi = sb("topi", [128, B, C, 8], U32)
        topf = sb("topf", [128, B, C, 8])
        ws1 = sb("ws1", [128, 2, D])
        ws1r = sb("ws1r", [128, 2, D], F32R)
        ws2 = sb("ws2", [128, D])
        bs1 = sb("bs1", [128, 1])
        hT_hi = [sb(f"hT_hi{b}", [128, T], F32R) for b in range(B)]
        hT_lo = [sb(f"hT_lo{b}", [128, T], F32R) for b in range(B)]
        wm = prob[0][:, 0, 0:6 * D]
        wmp = prob[0][:, 1, 0:2 * D]
        silb = prob[0][:, 2, 0:B * 128].rearrange("p (b k) -> p b k", b=B)
        hw = oT[:]
        rem = attn[:].rearrange("p c (k d) -> p (c k d)", k=2).rearrange("p (s t) -> p s t", s=2)
        free = part[:].rearrange("p b a s t -> p (b a s t)").bitcast(F32)
        cwb = [free[:, k * T:(k + 1) * T] for k in range(3)]
        cwT = free[0:E, 3 * T:5 * T].rearrange("e (b t) -> e b t", b=B)
        w1_raw, w1_hi = free[:, 0:(E + 1) * D], free[:, (E + 1) * D:2 * (E + 1) * D]
        w2_raw, w2_hi = free[:, 2 * (E + 1) * D:3 * (E + 1) * D], (hT_hi[1], hT_lo[1])
        hid = prob[0][:].rearrange("p q (a t) -> p (q a) t", t=CH)
        gat = prob[1][:].rearrange("p q (a t) -> p (q a) t", t=CH)

        with ExitStack() as operands:
            def operand(name, shape):
                return operands.enter_context(nc.sbuf_tensor(name, shape, BF16))

            qry = [operand(f"qry{j}", [KROWS, G, 2, T]) for j in range(2)]
            keys = [operand(f"keys{j}", [KROWS, G, T]) for j in range(2)]
        gat_hi = sb("gat_hi", [128, RING, CH], F32R)
        gat_lo = sb("gat_lo", [128, RING, CH], F32R)
        w2s = [sb(f"w2s_{k}", [128, 2, D]) for k in range(3)]
        w2r = [sb(f"w2r_{k}", [128, 2, D], F32R) for k in range(3)]
        ws2s = sb("ws2s", [128, 2, D])
        ws2r = sb("ws2r", [128, 2, D], F32R)

        slot = [ps(f"slot{k}", [128, T]) for k in range(SLOTS)]
        acc = ps("acc", [128, T])

        z_slot = [slot[0], slot[2]]
        sums = [acc, slot[2]]
        y_sums = [acc, slot[0]]
        up_bank = [slot[0][:, 0:CH], slot[0][:, CH:T], slot[1][:, 0:CH]]

        key_d = nc.dram_tensor("key_d", (NG, PARTS, HD, G, T), BF16, kind="Internal").ap()
        qry_d = nc.dram_tensor("qry_d", (NG, PARTS, HD, G, 2, T), BF16, kind="Internal").ap()
        shift_d = nc.dram_tensor("shift_d", (PARTS, HG, T), BF16, kind="Internal").ap()
        w2_d = nc.dram_tensor("w2_d", (E + 1, D, 2, D), F32, kind="Internal").ap()
        w1_d = nc.dram_tensor("w1_d", (E + 1, D, 2, D), F32, kind="Internal").ap()
        cw_d = nc.dram_tensor("cw_d", (B, E, T), F32, kind="Internal").ap()

        ld_c = sem("ld_c")
        ld_wm = sem("ld_wm")
        ld_x = [sem("ld_x0"), sem("ld_x1")]
        ld_ffn = sem("ld_ffn")
        consts = sem("consts")
        act_exp = sem("act_exp")
        silu_ok = sem("silu_ok")
        silb_ok = sem("silb_ok")
        wmp_ok = sem("wmp_ok")
        mod_mm = sem("mod_mm")
        mod_ok = sem("mod_ok")
        ca1_ok = sem("ca1_ok")
        aff_ok = sem("aff_ok")
        reach_ok = sem("reach_ok")
        z_ok = sem("z_ok")
        h_ok = sem("h_ok")
        hmod_ok = sem("hmod_ok")
        hT_mm = sem("hT_mm")
        hT_ok = sem("hT_ok")
        hw_ok = sem("hw_ok")
        rem_ok = sem("rem_ok")
        cut_a = sem("cut_a")
        cut_v = sem("cut_v")
        cut_p = [sem("cut_p0"), sem("cut_p1")]
        first_wr = [sem(f"first_wr{k}") for k in range(PARTS)]
        part_wr = [sem("part_wr0"), sem("part_wr1")]
        flag_ok = sem("flag_ok")
        ex_ld = sem("ex_ld")
        ex_mm = sem("ex_mm")
        ex_max = sem("ex_max")
        ex_seq = sem("ex_seq")
        shiftT_mm = sem("shiftT_mm")
        spart_ok = sem("spart_ok")
        shift_wr = sem("shift_wr")
        opnd = [sem("opnd0"), sem("opnd1")]
        first_q = [sem("first_q0"), sem("first_q1")]
        rest_go = sem("rest_go")
        val_ok = [sem("val_ok0"), sem("val_ok1")]
        filled = sem("filled")
        exp_done = sem("exp_done")
        pv_done = sem("pv_done")
        evac = sem("evac")
        norm_done = sem("norm_done")
        h2T_mm = sem("h2T_mm")
        h2T_ok = sem("h2T_ok")
        logit_mm = sem("logit_mm")
        lsub = sem("lsub")
        lexp = sem("lexp")
        cw_ok = sem("cw_ok")
        cwT_mm = sem("cwT_mm")
        cwT_ok = sem("cwT_ok")
        cw_wr = sem("cw_wr")
        raw_ld = sem("raw_ld")
        split_ok = sem("split_ok")
        split_wr = sem("split_wr")
        ld_ws1 = sem("ld_ws1")
        ld_ws2 = sem("ld_ws2")
        w2_ok = sem("w2_ok")
        ghi_ok = sem("ghi_ok")
        glo_ok = [sem("glo_ok0"), sem("glo_ok1")]
        h2s_ok = sem("h2s_ok")
        w1_ld = [sem(f"w1_ld{k}") for k in range(3)]
        ws1_ok = sem("ws1_ok")
        w1_ok = sem("w1_ok")
        w2_ld = [sem(f"w2_ld{k}") for k in range(3)]
        row_ld = [sem(f"row_ld{k}") for k in range(3)]
        l1_done = sem("l1_done")
        hid_ok = sem("hid_ok")
        gat_ok = sem("gat_ok")
        l2_done = sem("l2_done")
        ffT_ok = sem("ffT_ok")
        y_mm = sem("y_mm")
        y_ok = sem("y_ok")
        out_wr = sem("out_wr")
        dve_seq = sem("dve_seq")
        pool_seq = sem("pool_seq")

        block = ctx.enter_context(nc.Block())

        def uses(last=False, first=False):
            extra = {H2T_AT: "h2T", LOGIT_AT: "logit", CWT_AT: "cwT"} if last else {}
            told = []
            for j in range(2):
                section = [("score", j, u // G, u % G) for u in range(G * C)]
                section.insert(OUT_AT, ("none" if first and j == 0 else "turn", j, 0, 0))
                told += section
            for at in sorted(extra):
                told.insert(at, (extra[at], 0, 0, 0))
            return told

        FIRST, MIDDLE, LAST = uses(first=True), uses(), uses(last=True)

        def fill_count(it, r, body):
            return BODY * it - (0 if body is FIRST else 1) + sum(u[0] != "none" for u in body[:r + 1])

        def exp_count(it, units):
            return G * STEPS * it + units

        def pv_count(it, step, half):
            return HALVES * STEPS * it - HALVES + HALVES * step + half + 1

        def evac_count(it, j, half):
            return 2 * HALVES * it - HALVES + HALVES * j + half + 1

        def norm_count(it, j):
            return 2 * it + j

        def chunk(b, m, q):
            return FALL * b + FCH * m + q

        def place(b, k):
            return FCH * ((k + b) % 3)

        def exact_wanted(eng):
            eng.wait_ge(flag_ok, 1)
            return eng.value_load(flag[0:1, 0:1], min_val=0, max_val=1)

        OPND_LOADS = KEY_LOADS + QUERY_LOADS + SHIFT_LOADS
        PART_WRITES = 2 * PARTS

        def write_part(eng, b, p, lo, hi, signal):
            n = HALVES * b + HALVES - 1
            if b == 0:
                eng.wait_ge(cut_v, 3 * n + p + 1)
                eng.wait_ge(cut_a, (3, 4, 4)[p])
            else:
                eng.wait_ge(cut_v, 3 * n + (2, 3, 3)[p])
            if p == PARTS - 1:
                eng.wait_ge(cut_p[b], HALVES)
            src = part[32 * lo:32 * hi, b, p]
            lo, hi = NG // B * b + lo, NG // B * b + hi
            eng.dma_start(key_d[lo:hi, p].rearrange("n d q t -> n (d q) t"), src[:, 0]).then_inc(signal, 16)
            eng.dma_start(qry_d[lo:hi, p].rearrange("n d q s t -> n (d q) (s t)"),
                          src.rearrange("f s t -> f (s t)")).then_inc(signal, 16)

        def write_shift(eng):
            eng.dma_start(shift_d.rearrange("p (b h) (c m) -> p b (h c) m", b=B, c=C).rearrange("p b q m -> q p b m"),
                          spart[:].rearrange("q p (b m) -> q p b m", b=B)).then_inc(shift_wr, 16)

        def in_groups(row):
            return row.rearrange("p (n q d) -> p n d q", q=G, d=HD)

        def grouped(row):
            return row.rearrange("p (n d q) -> p n d q", q=G, d=HD)

        def over_classes(row):
            return row.unsqueeze(1).broadcast_to((128, C, D))

        def cols(b):
            return slice(b * D, (b + 1) * D)

        def experts(eng, b, lo, hi, work):
            if hi - lo > 1:
                with eng.Fori(lo, hi) as i:
                    for k in range(3):
                        work(i, k)
            else:
                for k in range(3):
                    work(lo, k)

        @block.sync
        def _(sp):
            with nc.allow_non_contiguous_dma(reason="small transposed vectors"):
                sp.dma_start(cT[:], cvec.rearrange("b d -> d b")).then_inc(ld_c, 16)
                sp.dma_start(x_sb[:, :, cols(0)], x[0].rearrange("(m c) d -> m c d", c=C)).then_inc(ld_x[0], 16)
                sp.dma_start(wcol[:, 0:1], ipw.partition_broadcast(128)).then_inc(ld_c, 16)
                sp.dma_start(wm[:], wmod).then_inc(ld_wm, 16)
                sp.dma_start(x_sb[:, :, cols(1)], x[1].rearrange("(m c) d -> m c d", c=C)).then_inc(ld_x[1], 16)
                sp.dma_start(rw[:], router_w).then_inc(ld_ffn, 16)
                sp.dma_start(rb[:], router_b.partition_broadcast(128)).then_inc(ld_ffn, 16)
                sp.dma_start(b2c[:, 0:1], sb2.rearrange("(h o) -> h o", o=1)).then_inc(ld_ffn, 16)
                sp.dma_start(b2r[:], eb2).then_inc(ld_ffn, 16)
                sp.dma_start(ws2[:], sw2).then_inc(ld_ffn, 16)
                sp.dma_start(bs1[:], sb1.rearrange("(h o) -> h o", o=1)).then_inc(ld_ffn, 16)

            def load_key_part(dst, n, a, signal):
                at = HD * PARTS * a
                src = key_d[bass.ds(n, 1), a].rearrange("n d q t -> n d (q t)")
                sp.dma_start(dst[at:at + PARTS * HD].rearrange("k q t -> k (q t)"),
                             src.broadcast_to((PARTS, HD, G * T))).then_inc(signal, 16)

            def load_keys(dst, n, signal):
                for a in range(PARTS):
                    load_key_part(dst, n, a, signal)

            def load_queries(dst, n, signal, lo=0, hi=G):
                src = qry_d[bass.ds(n, 1)].rearrange("n p d q s t -> n (p d) (q s t)")
                sp.dma_start(dst[0:ROWS, lo:hi].rearrange("k q s t -> k (q s t)"),
                             src[:, :, 2 * T * lo:2 * T * hi].broadcast_to((PARTS, PARTS * HD, (hi - lo) * 2 * T))
                             ).then_inc(signal, 16)

            def load_shift(n, j, signal):
                for s in range(2):
                    sp.dma_start(qry[j][ROWS:KROWS, :, s], shift_d[:, bass.ds(G * n, G)]).then_inc(signal, 16)

            def load_group(it, j):
                n = 2 * it + j
                load_shift(n, j, opnd[j])
                load_keys(keys[j], n, opnd[j])
                load_queries(qry[j], n, opnd[j])

            for p in range(PARTS):
                write_part(sp, 0, p, 0, 1, first_wr[p])

            def wait_first_parts(n):
                for p in range(n):
                    sp.wait_ge(first_wr[p], 32)

            exact = exact_wanted(sp)
            with sp.If(exact > 0):
                sp.sem_inc(rest_go, 1)
                wait_first_parts(PARTS)
                for b in range(B):
                    sp.wait_ge(part_wr[b], 16 * PART_WRITES)
                with sp.Fori(0, NG) as n:
                    sp.wait_ge(ex_max, G * C * n + C)
                    load_keys(keys[0], n, ex_ld)
                    load_queries(qry[0], n, ex_ld)
                sp.wait_ge(ex_max, C * HG + C)
                sp.wait_ge(shift_wr, 16)
                sp.wait_ge(spart_ok, 2)
                write_shift(sp)
                sp.wait_ge(shift_wr, 32)

            sp.wait_ge(consts, 5)
            for p in range(PARTS):
                sp.wait_ge(first_wr[p], 32)
                load_key_part(keys[0], 0, p, opnd[0])
            load_queries(qry[0], 0, first_q[0], 0, G // 2)
            sp.wait_ge(shift_wr, 16)
            load_shift(0, 0, opnd[0])
            load_queries(qry[0], 0, first_q[1], G // 2, G)
            sp.sem_inc(rest_go, 1)
            sp.wait_ge(part_wr[0], 16 * PART_WRITES)
            load_group(0, 1)
            def load_first_layer(e, k):
                sp.dma_start(w1[k][:], w1_d[e]).then_inc(w1_ld[k], 16)
                sp.dma_start(b1[k][:], eb1[e].rearrange("(h o) -> h o", o=1)).then_inc(w1_ld[k], 16)

            def load_second_layer(b, e, k):
                if b:
                    sp.dma_start(w2s[k][:], w2_d[e]).then_inc(w2_ld[k], 16)
                else:
                    sp.dma_start(w2[k][:], ew2[e]).then_inc(w2_ld[k], 16)

            for k in range(3):
                load_second_layer(0, k, k)
            sp.wait_ge(part_wr[1], 16 * PART_WRITES)
            sp.dma_start(w1_raw[:, 0:E * D].rearrange("d (e h) -> d e h", e=E), ew1.rearrange("e d h -> d e h")
                         ).then_inc(raw_ld, 16)
            sp.dma_start(w1_raw[:, E * D:], sw1).then_inc(raw_ld, 16)
            sp.dma_start(w2_raw[:, 0:E * D].rearrange("d (e h) -> d e h", e=E), ew2.rearrange("e d h -> d e h")
                         ).then_inc(raw_ld, 16)
            sp.dma_start(w2_raw[:, E * D:], sw2).then_inc(raw_ld, 16)
            with sp.Fori(1, ITERS) as it:
                for j in range(2):
                    sp.wait_ge(filled, BODY * it + SEC * (j + 1) - 1 - BODY)
                    load_group(it, j)

            sp.wait_ge(split_wr, 16 * 5)
            sp.dma_start(ws1[:], w1_d[E]).then_inc(ld_ws1, 16)
            for k in range(3):
                load_first_layer(k, k)

            def load_row(b, e, k):
                sp.dma_start(cwb[k], cw_d[b, bass.ds(e, 1), :].broadcast_to((128, T))).then_inc(row_ld[k], 16)

            def load_expert(b, i, k, first=False):
                before = chunk(0, E - 2 + k, FCH - 1) if first else chunk(b, 3 * i + k - 2, FCH - 1)
                if not (first and k == 0):
                    sp.wait_ge(hid_ok, UPB + before + 1)
                    load_first_layer(3 * i + k, k)
                sp.wait_ge(gat_ok, RING + before + 1)
                load_row(b, 3 * i + k, k)
                sp.wait_ge(l2_done, RING + before + 1)
                load_second_layer(b, 3 * i + k, k)

            for b in range(B):
                if b:
                    sp.wait_ge(filled, BODY * ITERS + 3)
                    sp.dma_start(ws2s[:], w2_d[E]).then_inc(ld_ws2, 16)
                    sp.wait_ge(hid_ok, UPB + chunk(0, E - 2, FCH - 1) + 1)
                    load_first_layer(0, 0)
                sp.wait_ge(cwT_ok, b + 1)
                sp.dma_start(cw_d[b], cwT[:, b]).then_inc(cw_wr, 16)
                sp.wait_ge(cw_wr, 16 * b + 16)
                for k in range(3):
                    if b:
                        load_expert(b, 0, k, first=True)
                    else:
                        load_row(b, k, k)
                with sp.Fori(1, E // 3) as i:
                    for k in range(3):
                        load_expert(b, i, k)

            out_v = out.rearrange("b (m c) d -> b m c d", c=C)
            for b in range(B):
                for half in range(HALVES):
                    lo, hi = half * C // HALVES, (half + 1) * C // HALVES
                    sp.wait_ge(y_ok, HALVES * b + half + 1)
                    sp.dma_start(out_v[b, :, lo:hi], h_sb[:, lo:hi, cols(b)]).then_inc(out_wr, 16)
            sp.wait_ge(out_wr, 16 * B * HALVES)

        @block.gpsimd
        def _(pool):
            pool.sem_inc(gat_ok, RING)
            nc.gpsimd.memset(ones[:], 1.0).then_inc(consts, 1)
            nc.gpsimd.memset(ident[:], 0.0).then_inc(pool_seq, 1)
            pool.wait_ge(pool_seq, 1)
            nc.gpsimd.affine_select(out=ident[:], in_=ident[:], compare_op=ALU.not_equal, fill=1.0, base=0,
                                    pattern=[[-1, 128]], channel_multiplier=1).then_inc(consts, 1)
            nc.gpsimd.iota(iota[:], [[1, E]], base=0, channel_multiplier=0,
                           allow_small_or_imprecise_dtypes=True).then_inc(consts, 1)
            for j in range(2):
                nc.gpsimd.memset(val[j][:], 0.0).then_inc(pool_seq, 1)
            pool.wait_ge(pool_seq, 3)
            for j in range(2):
                last = nc.gpsimd.memset(val[j][:, :, :, HD:HD + 1], 1.0)
            last.then_inc(consts, 1)
            for j in range(2):
                last = nc.gpsimd.memset(keys[j][:], 1.0)
            last.then_inc(consts, 1)

            def copy_values(it, j):
                at = 2 * G * HD * it + G * HD * j
                nc.gpsimd.tensor_copy(val[j][:, :, :, 0:HD],
                                      h_sb[:, :, bass.ds(at, G * HD)].rearrange("m c (d q) -> m c q d", q=G)
                                      ).then_inc(val_ok[j], 1)

            def modulate(b):
                pool.wait_ge(hT_mm, HALVES * (b + 1))
                h_b = h_sb[:, :, cols(b)]
                if b == 0:
                    third_part(0)
                nc.gpsimd.tensor_tensor(h_b, h_b, over_classes(mod[:, 1, cols(b)]), ALU.mult).then_inc(hmod_ok, 1)
                if b == 0:
                    third_part(1)
                pool.wait_ge(hmod_ok, 2 * b + 1)
                nc.gpsimd.tensor_tensor(h_b, h_b, over_classes(mod[:, 0, cols(b)]), ALU.add).then_inc(hmod_ok, 1)

            def third_part(half):
                at = slice(half * CH, (half + 1) * CH)
                pool.wait_ge(cut_a, 2 * half + 2)
                nc.gpsimd.tensor_tensor(part[:, 0, 2, 1, at], rem[:, 1, at], part[:, 0, 1, 1, at],
                                        ALU.subtract).then_inc(cut_p[0], 1)

            pool.wait_ge(ca1_ok, 1)
            modulate(0)
            pool.wait_ge(consts, 5)
            pool.wait_ge(hmod_ok, 2)
            for j in range(2):
                copy_values(0, j)
            pool.wait_ge(rest_go, 1)
            for p in range(PARTS):
                write_part(pool, 0, p, 1, NG // B, part_wr[0])
            modulate(1)
            for p in range(PARTS):
                write_part(pool, 1, p, 0, NG // B, part_wr[1])
            pool.wait_ge(hmod_ok, 4)
            pool.wait_ge(split_ok, 2)
            for s, w in enumerate((w1_hi, w1_raw)):
                pool.dma_start(w1_d[:, :, s].rearrange("e d h -> d e h"), w.rearrange("d (e h) -> d e h", h=D)
                             ).then_inc(split_wr, 16)
            pool.wait_ge(split_ok, 2 + HALVES + 1)
            pool.dma_start(w2_d[:, :, 1].rearrange("e d h -> d e h"), w2_raw.rearrange("d (e h) -> d e h", h=D)
                         ).then_inc(split_wr, 16)
            for half, w in enumerate(w2_hi):
                e = (E + 1) // 2 * half
                pool.dma_start(w2_d[e:e + (E + 1) // 2, :, 0].rearrange("e d h -> d e h"),
                             w[:].bitcast(F32).rearrange("d (e h) -> d e h", h=D)).then_inc(split_wr, 16)
            with pool.Fori(1, ITERS) as it:
                for j in range(2):
                    pool.wait_ge(pv_done, pv_count(it, -C if j == 0 else 0, HALVES - 1))
                    copy_values(it, j)

            for q in range(FCH):
                at = place(0, -1) + q
                pool.wait_ge(hid_ok, UPB + q + 1)
                nc.gpsimd.tensor_tensor(gat[:, at], hid[:, at], ones[:, 0:1].broadcast_to((128, CH)),
                                        ALU.mult).then_inc(gat_ok, 1)

            def weight(i, k):
                pool.wait_ge(row_ld[k], 16 * (i + 1))
                for q in range(FCH):
                    n, at = chunk(0, 3 * i + k + 1, q), place(0, k) + q
                    pool.wait_ge(hid_ok, UPB + n + 1)
                    pool.wait_ge(l2_done, n + 1)
                    nc.gpsimd.tensor_tensor(gat[:, at], hid[:, at], cwb[k][:, q * CH:(q + 1) * CH],
                                            ALU.mult).then_inc(gat_ok, 1)

            experts(pool, 0, 0, E // 3, weight)

            def low_part(m, at):
                pool.wait_ge(ghi_ok, FCH * m + 1)
                nc.gpsimd.tensor_tensor(gat_lo[:, at], gat[:, at], gat_hi[:, at].bitcast(F32),
                                        ALU.subtract).then_inc(glo_ok[0], 1)

            low_part(0, place(1, -1))
            experts(pool, 1, 0, E // 3, lambda i, k: low_part(3 * i + k + 1, place(1, k)))

        @block.scalar
        def _(act):
            act.sem_inc(hid_ok, UPB)
            act.wait_ge(ld_c, 32)
            nc.scalar.activation(sil[:, 0], cT[:], ACT.Exp, scale=-1.0).then_inc(act_exp, 1)
            nc.scalar.activation(wcol[:, 1:2], wcol[:, 0:1], ACT.Exp, scale=-1.0).then_inc(act_exp, 1)

            act.wait_ge(ld_wm, 16)
            nc.scalar.activation(grouped(wmp[:]), in_groups(wm[:, 0:2 * D]), ACT.Copy).then_inc(wmp_ok, 1)

            act.wait_ge(consts, 2)
            act.wait_ge(silu_ok, 1)
            for b in range(B):
                nc.scalar.activation(silb[:, b], ones[:], ACT.Copy, scale=sil[:, 3, b:b + 1]).then_inc(silb_ok, 1)

            act.wait_ge(mod_mm, 1)
            nc.scalar.activation(modT[:].rearrange("p k b -> p (k b)"), slot[2][:, CH:CH + 3 * B],
                                 ACT.Copy).then_inc(mod_ok, 1)
            nc.scalar.activation(mod[:, 0:2], acc[:, 0:CH], ACT.Copy).then_inc(mod_ok, 1)

            act.wait_ge(aff_ok, 1)
            for b in range(B):
                for half in range(HALVES):
                    act.wait_ge(hT_mm, HALVES * b + half + 1)
                    at = slice(half * CH, (half + 1) * CH)
                    nc.scalar.activation(hT[:, b * T + half * CH:b * T + (half + 1) * CH], z_slot[b][:, at],
                                         ACT.Identity, bias=modT[:, 0, b:b + 1], scale=aff[:, 0, b:b + 1]
                                         ).then_inc(hT_ok, 1)
                    if b == 0:
                        nc.scalar.activation(hw[:, at], z_slot[b][:, at], ACT.Identity, bias=aff[:, 2, b:b + 1],
                                             scale=aff[:, 1, b:b + 1]).then_inc(hw_ok, 1)
                        act.wait_ge(hw_ok, half + 1)
                        nc.scalar.activation(part[:, b, 0, 1, at], hw[:, at], ACT.Copy).then_inc(cut_a, 1)
                        if half == 0:
                            act.wait_ge(mod_mm, 2)
                            nc.scalar.activation(mod[:, 2:4], acc[:, CH:T], ACT.Copy).then_inc(mod_ok, 1)
                            nc.scalar.activation(mod[:, 4], slot[2][:, 0:B * D], ACT.Copy).then_inc(mod_ok, 1)
                        act.wait_ge(rem_ok, half + 1)
                        nc.scalar.activation(part[:, b, 1, 1, at], rem[:, 1, at], ACT.Copy).then_inc(cut_a, 1)
                if b == 0:
                    act.wait_ge(reach_ok, 1)
                    nc.scalar.activation(spart[:], spart1[:].unsqueeze(2).broadcast_to((128, PARTS, B * 128)),
                                         ACT.Copy).then_inc(spart_ok, 1)
                    act.wait_ge(spart_ok, 1)
                    write_shift(act)

            def h2_to_sbuf(b, src):
                nc.scalar.activation(hT[:, b * T:(b + 1) * T], src[:], ACT.Copy).then_inc(h2T_ok, 1)

            def exp_logits(b):
                act.wait_ge(lsub, b + 1)
                nc.scalar.activation(lg[:, b, 1], lg[:, b, 0], ACT.Exp).then_inc(lexp, 1)

            def weights_to_sbuf(b, src):
                act.wait_ge(split_wr, 16 * 5)
                nc.scalar.activation(cwT[:, b], src[0:E, :], ACT.Copy).then_inc(cwT_ok, 1)

            def exps(it, body):
                for r, (kind, j, c, q) in enumerate(body):
                    if kind in ("none", "turn", "logit"):
                        continue
                    act.wait_ge(filled, fill_count(it, r, body))
                    if kind == "h2T":
                        h2_to_sbuf(0, slot[r % SLOTS])
                    elif kind == "cwT":
                        weights_to_sbuf(0, slot[r % SLOTS])
                    else:
                        step = C * j + c
                        if q == 0 and not (body is FIRST and step < 2):
                            act.wait_ge(pv_done, pv_count(it, step - 1, HALVES - 1))
                        nc.scalar.activation(prob[c % 2][:, q, :], slot[r % SLOTS][:], ACT.Exp,
                                             scale=SCALE).then_inc(exp_done, 1)
                    if body is LAST and r == LOGIT_AT + 4:
                        exp_logits(0)

            exps(0, FIRST)
            with act.Fori(1, ITERS - 1) as it:
                exps(it, MIDDLE)
            exps(ITERS - 1, LAST)

            def hidden(b, m, at, bias):
                for q in range(FCH):
                    n = chunk(b, m, q)
                    act.wait_ge(l1_done, n + 1)
                    act.wait_ge(gat_ok, n + 1)
                    nc.scalar.activation(hid[:, at + q], up_bank[(at + q) % UPB], ACT.Relu,
                                         bias=bias).then_inc(hid_ok, 1)

            def gated(b):
                for q in range(FCH):
                    act.wait_ge(l2_done, RING + chunk(b, E, q) + 1)
                    nc.scalar.activation(hT[:, b * T + q * CH:b * T + (q + 1) * CH], sums[b][:, q * CH:(q + 1) * CH],
                                         ACT.Identity, bias=gbT[:, 3, b:b + 1], scale=gbT[:, 2, b:b + 1]
                                         ).then_inc(ffT_ok, 1)

            def to_f32r(b, i, k):
                act.wait_ge(w1_ld[k], 32 * (E // 3 * b + i + 1))
                nc.scalar.activation(w1r[k][:], w1[k][:], ACT.Copy).then_inc(w1_ok, 1)

            def routed(b, i, k):
                hidden(b, 3 * i + k + 1, place(b, k), b1[k][:])
                if b:
                    second_to_f32r(i, k)
                to_f32r(b, i + (k + 2) // 3, (k + 2) % 3)

            def second_to_f32r(i, k):
                act.wait_ge(w2_ld[k], 16 * (E // 3 + i + 1))
                nc.scalar.activation(w2r[k][:], w2s[k][:], ACT.Copy).then_inc(w2_ok, 1)

            act.wait_ge(ld_ws1, 16)
            nc.scalar.activation(ws1r[:], ws1[:], ACT.Copy).then_inc(ws1_ok, 1)
            to_f32r(0, 0, 0)
            to_f32r(0, 0, 1)
            hidden(0, 0, place(0, -1), bs1[:])

            def routed0(i, k):
                routed(0, i, k)

            experts(act, 0, 0, 2, routed0)
            routed0(2, 0)
            act.wait_ge(h2T_mm, 1)
            h2_to_sbuf(1, slot[2])
            routed0(2, 1)
            routed0(2, 2)
            routed0(3, 0)
            exp_logits(1)
            routed0(3, 1)
            routed0(3, 2)
            routed0(4, 0)
            act.wait_ge(cwT_mm, 1)
            weights_to_sbuf(1, slot[2])
            routed0(4, 1)
            routed0(4, 2)
            act.wait_ge(ld_ws2, 16)
            nc.scalar.activation(ws2r[:], ws2s[:], ACT.Copy).then_inc(w2_ok, 1)
            hidden(1, 0, place(1, -1), bs1[:])
            routed(1, 0, 0)
            gated(0)
            routed(1, 0, 1)
            routed(1, 0, 2)
            experts(act, 1, 1, E // 3 - 1, lambda i, k: routed(1, i, k))
            routed(1, E // 3 - 1, 0)
            for k in range(1, 3):
                hidden(1, E - 2 + k, place(1, k), b1[k][:])
                second_to_f32r(E // 3 - 1, k)
            gated(1)

        @block.vector
        def _(dve):
            seq = [0]
            v = nc.vector

            def link(ins):
                seq[0] += 1
                ins.then_inc(dve_seq, 1)
                dve.wait_ge(dve_seq, seq[0])

            dve.wait_ge(act_exp, 2)
            link(v.tensor_scalar(sil[:, 1], sil[:, 0], 1.0, None, ALU.add))
            link(v.reciprocal(sil[:, 2], sil[:, 1]))
            v.tensor_tensor(sil[:, 3], sil[:, 2], cT[:], ALU.mult).then_inc(silu_ok, 1)

            def moments(src, b, lo=0, hi=C):
                for c in range(lo, hi):
                    last = v.bn_stats(stats[:, b, c], src[:, c, cols(b)])
                return last

            def statistics(b):
                for c in range(C):
                    last = v.bn_aggr(mv[:, b, c], stats[:, b, c])
                link(last)
                var, y, t = rstd[:, b, 0], rstd[:, b, 1], rstd[:, b, 2]
                link(v.tensor_scalar(var, mv[:, b, :, 1], EPS, None, ALU.add))
                link(v.tensor_scalar(rint[:, b, 0], var.bitcast(I32), 1, None, ALU.logical_shift_right))
                link(v.tensor_scalar(rint[:, b, 1], rint[:, b, 0], -1.0, float(0x5F3759DF), ALU.mult, ALU.add))
                for guess in (rint[:, b, 1].bitcast(F32), y, y):
                    link(v.tensor_tensor(t, guess, guess, ALU.mult))
                    link(v.scalar_tensor_tensor(t, t, -0.5, var, ALU.mult, ALU.mult))
                    link(v.scalar_tensor_tensor(y, t, 1.5, guess, ALU.add, ALU.mult))

            def normalised(src, b, reorder=False, lo=0, hi=C):
                for c in range(lo, hi):
                    z_c, x_c = h_sb[:, c, cols(b)], src[:, c, cols(b)]
                    if reorder:
                        z_c, x_c = grouped(z_c), in_groups(x_c)
                    last = v.tensor_scalar(z_c, x_c, mv[:, b, c, 0:1],
                                           rstd[:, b, 1, c:c + 1], ALU.subtract, ALU.mult)
                return last

            def modulated(b, add_row, mul_row):
                h_b = h_sb[:, :, cols(b)]
                link(v.tensor_tensor(h_b, h_b, over_classes(mod[:, mul_row, cols(b)]), ALU.mult))
                return v.tensor_tensor(h_b, h_b, over_classes(mod[:, add_row, cols(b)]), ALU.add)

            def gate(dst, tmp):
                link(v.tensor_scalar(tmp, dst, -1.0, 0.25, ALU.mult, ALU.max))
                link(v.tensor_tensor(tmp, tmp, dst, ALU.max))
                link(v.tensor_scalar(dst, dst, 0.0, 2.0, ALU.is_ge, ALU.mult))
                link(v.scalar_tensor_tensor(dst, dst, -1.0, tmp, ALU.add, ALU.mult))

            def cut(b):
                for half in range(HALVES):
                    at = slice(half * CH, (half + 1) * CH)
                    src = hT[:, b * T + half * CH:b * T + (half + 1) * CH]
                    n = HALVES * b + half
                    dve.wait_ge(hT_ok, n + 1)
                    v.tensor_copy(part[:, b, 0, 0, at], src).then_inc(cut_v, 1)
                    if b:
                        link(v.tensor_scalar(hw[:, at], src, wcol[:, 2:3], None, ALU.mult))
                        link(v.tensor_copy(part[:, b, 0, 1, at], hw[:, at]))
                        dve.wait_ge(cut_p[0], half + 1)
                    elif half == 0:
                        link(moments(x_sb, 1, C // 2, C))
                    if b == 0:
                        dve.wait_ge(cut_a, 2 * n + 1)
                    v.tensor_tensor(rem[:, 1, at], hw[:, at], part[:, b, 0, 1, at], ALU.subtract).then_inc(rem_ok, 1)
                    dve.wait_ge(cut_v, 3 * n + 1)
                    link(v.tensor_tensor(rem[:, 0, at], src, part[:, b, 0, 0, at], ALU.subtract))
                    v.tensor_copy(part[:, b, 1, 0, at], rem[:, 0, at]).then_inc(cut_v, 1)
                    if b:
                        dve.wait_ge(rem_ok, n + 1)
                        link(v.tensor_copy(part[:, b, 1, 1, at], rem[:, 1, at]))
                    dve.wait_ge(cut_v, 3 * n + 2)
                    v.tensor_tensor(part[:, b, 2, 0, at], rem[:, 0, at], part[:, b, 1, 0, at],
                                    ALU.subtract).then_inc(cut_v, 1)
                    if b:
                        v.tensor_tensor(part[:, b, 2, 1, at], rem[:, 1, at], part[:, b, 1, 1, at],
                                        ALU.subtract).then_inc(cut_p[1], 1)

            dve.wait_ge(ld_x[0], 16)
            v.tensor_scalar(wcol[:, 1:2], wcol[:, 1:2], 1.0, None, ALU.add)
            link(moments(x_sb, 0))
            v.reciprocal(wcol[:, 2:3], wcol[:, 1:2])
            statistics(0)
            dve.wait_ge(mod_ok, 1)
            v.tensor_scalar(aff[:, 0], modT[:, 1], 1.0, None, ALU.add)
            normalised(x_sb, 0, True, 0, C // 2).then_inc(z_ok, 1)
            dve.wait_ge(z_ok, 1)
            v.tensor_scalar(aff[:, 1], aff[:, 0], wcol[:, 2:3], None, ALU.mult)
            v.tensor_scalar(aff[:, 2], modT[:, 0], wcol[:, 2:3], None, ALU.mult).then_inc(aff_ok, 1)
            normalised(x_sb, 0, True, C // 2, C).then_inc(z_ok, 1)
            dve.wait_ge(mod_ok, 2)
            v.tensor_scalar(mod[:, 1], mod[:, 1], 1.0, None, ALU.add).then_inc(ca1_ok, 1)
            dve.wait_ge(ld_x[1], 16)
            moments(x_sb, 1, 0, C // 2)
            cut(0)

            v.tensor_reduce(reach[:, 1:2], mod[:, 0], AX.X, ALU.max, apply_absolute_value=True)
            link(v.tensor_reduce(reach[:, 0:1], mod[:, 1], AX.X, ALU.max, apply_absolute_value=True))
            link(v.tensor_scalar(reach[:, 2:3], reach[:, 1:2], float(HD) ** 0.5, None, ALU.mult))
            link(v.scalar_tensor_tensor(reach[:, 3:4], reach[:, 0:1], float(D) ** 0.5, reach[:, 2:3], ALU.mult, ALU.add))
            link(v.scalar_tensor_tensor(reach[:, 4:5], reach[:, 3:4], -ROUNDING, reach[:, 3:4], ALU.mult, ALU.mult))
            limit = 1.0 if force_exact else -SAFE_EXPONENT / SCALE
            v.tensor_scalar(flag[:], reach[:, 4:5], limit, None, ALU.is_lt).then_inc(flag_ok, 1)
            link(v.tensor_copy(spart1[:, 0:1], reach[:, 4:5]))
            link(v.tensor_tensor(reach[:, 5:6], reach[:, 4:5], spart1[:, 0:1], ALU.subtract))
            link(v.tensor_copy(spart1[:, 1:2], reach[:, 5:6]))
            v.tensor_tensor(spart1[:, 2:3], reach[:, 5:6], spart1[:, 1:2], ALU.subtract).then_inc(reach_ok, 1)

            statistics(1)
            normalised(x_sb, 1, True, 0, C // 2).then_inc(z_ok, 1)
            normalised(x_sb, 1, True, C // 2, C).then_inc(z_ok, 1)
            cut(1)

            exact = exact_wanted(dve)
            with dve.If(exact > 0):
                dve.sem_inc(ex_max, C)
                with dve.Fori(0, NG) as n:
                    for u in range(G * C):
                        dve.wait_ge(ex_mm, G * C * n + u + 1)
                        v.reduce_max(shift[:].rearrange("p g c -> p (g c)")[:, bass.ds(G * C * n + u, 1)],
                                     slot[u % 2][:], AX.X, negate=True).then_inc(ex_max, 1)
                dve.wait_ge(shiftT_mm, 1)
                dve.wait_ge(shift_wr, 16)
                sT = acc[:, 0:B * 128]
                v.tensor_copy(spart[:, 0], sT).then_inc(ex_seq, 1)
                dve.wait_ge(ex_seq, 1)
                v.tensor_tensor(srem[:], sT, spart[:, 0], ALU.subtract).then_inc(ex_seq, 1)
                dve.wait_ge(ex_seq, 2)
                v.tensor_copy(spart[:, 1], srem[:]).then_inc(ex_seq, 1)
                dve.wait_ge(ex_seq, 3)
                v.tensor_tensor(spart[:, 2], srem[:], spart[:, 1], ALU.subtract).then_inc(spart_ok, 1)

            dve.wait_ge(mod_ok, 4)
            v.tensor_copy(gbT[:, 0], modT[:, 2])
            link(v.tensor_scalar(mod[:, 4], mod[:, 4], 1.0, None, ALU.add))
            gate(mod[:, 2], modt[:])
            gate(gbT[:, 0], gbT[:, 1])
            dve.wait_ge(ld_ffn, 96)
            link(v.tensor_copy(gbT[:, 2], gbT[:, 0]))
            link(v.tensor_scalar(gbT[:, 3], gbT[:, 0], b2c[:, 0:1], None, ALU.mult))

            def split_weights():
                dve.wait_ge(raw_ld, 64)
                v.tensor_copy(w1_hi.bitcast(F32R), w1_raw).then_inc(split_ok, 1)
                dve.wait_ge(split_ok, 1)
                v.tensor_tensor(w1_raw.bitcast(F32R), w1_raw, w1_hi, ALU.subtract).then_inc(split_ok, 1)
                for half, hi in enumerate(w2_hi):
                    v.tensor_copy(hi[:], w2_raw[:, half * T:(half + 1) * T]).then_inc(split_ok, 1)
                dve.wait_ge(split_ok, 2 + HALVES)
                for half, hi in enumerate(w2_hi):
                    raw = w2_raw[:, half * T:(half + 1) * T]
                    last = v.tensor_tensor(raw.bitcast(F32R), raw, hi[:].bitcast(F32), ALU.subtract)
                last.then_inc(split_ok, 1)

            def split_rows(b):
                src = hT[:, b * T:(b + 1) * T]
                dve.wait_ge(h2T_ok, b + 1)
                dve.wait_ge(split_wr, 16 * 5)
                link(v.tensor_copy(hT_hi[b][:], src))
                v.tensor_tensor(hT_lo[b][:], src, hT_hi[b][:].bitcast(F32), ALU.subtract).then_inc(h2s_ok, 1)

            def take_sums(it, j):
                for half in range(HALVES):
                    dve.wait_ge(pv_done, pv_count(it, C * j, half))
                    v.tensor_copy(oT[:, half * CH:(half + 1) * CH],
                                  acc[:, half * CH:(half + 1) * CH]).then_inc(evac, 1)

            def divide(it, j, count, src):
                dve.wait_ge(filled, count)
                sums = src[:].rearrange("m (c q k) -> m c q k", c=C, q=G)
                link(v.reciprocal(rden[:], sums[:, :, :, HD]))
                at = G * HD * (2 * it + j - 1)
                v.tensor_tensor(attn[:, :, at:at + G * HD].rearrange("m c (q d) -> m c q d", q=G),
                                sums[:, :, :, 0:HD], rden[:].unsqueeze(3).broadcast_to((128, C, G, HD)),
                                ALU.mult).then_inc(norm_done, 1)

            def residual(b):
                a = attn[:, :, cols(b)]
                link(v.tensor_tensor(a, a, over_classes(mod[:, 2, cols(b)]), ALU.mult))
                link(v.tensor_tensor(a, a, x_sb[:, :, cols(b)], ALU.add))

            def route(b, src):
                def over_tiles(row):
                    return row.unsqueeze(1).broadcast_to((128, C, E))

                def over_experts(col):
                    return col.unsqueeze(2).broadcast_to((128, C, E))

                l0, l1, l2, l3 = (lg[:, b, k] for k in range(4))
                link(v.tensor_tensor(l0, src[:, 0:16 * C].rearrange("p (t e) -> p t e", e=16)[:, :, 0:E],
                                     over_tiles(rb[:]), ALU.add))
                link(v.reduce_max(lred[:, b, 0], l0, AX.X))
                v.tensor_tensor(l0, l0, over_experts(lred[:, b, 0]), ALU.subtract).then_inc(lsub, 1)
                dve.wait_ge(lexp, b + 1)
                link(v.tensor_reduce(lred[:, b, 1], l1, AX.X, ALU.add))
                link(v.reciprocal(lred[:, b, 2], lred[:, b, 1]))
                link(v.tensor_tensor(l0, l1, over_experts(lred[:, b, 2]), ALU.mult))
                for c in range(C):
                    last = v.max(top[:, b, c], l0[:, c])
                link(last)
                for c in range(C):
                    last = v.max_index(topi[:, b, c], top[:, b, c], l0[:, c])
                link(last)
                link(v.tensor_copy(topf[:, b], topi[:, b]))
                link(v.tensor_tensor(l1, over_tiles(iota[:]), over_experts(topf[:, b, :, 0]), ALU.is_equal))
                for k in range(1, K):
                    link(v.tensor_tensor(l2, over_tiles(iota[:]), over_experts(topf[:, b, :, k]), ALU.is_equal))
                    link(v.tensor_tensor(l1, l1, l2, ALU.add))
                v.tensor_tensor(l3, l0, l1, ALU.mult).then_inc(cw_ok, 1)

            for it in range(ITERS):
                body = FIRST if it == 0 else LAST if it == ITERS - 1 else MIDDLE
                for j in range(2):
                    if it + j == 0:
                        continue
                    take_sums(it, j)
                    r = body.index(("turn", j, 0, 0))
                    divide(it, j, fill_count(it, r, body), slot[r % SLOTS])
                    if (it, j) == (0, 1):
                        split_weights()
                    if (it, j) == (ITERS // 2, 0):
                        dve.wait_ge(norm_done, norm_count(it, j))
                        residual(0)
                        link(moments(attn, 0))
                        statistics(0)
                        link(normalised(attn, 0))
                        modulated(0, 3, 4).then_inc(h_ok, 1)
                    if (it, j) == (ITERS - 1, 0):
                        r = body.index(("logit", 0, 0, 0))
                        dve.wait_ge(filled, fill_count(it, r, body))
                        route(0, slot[r % SLOTS])
                        split_rows(0)
            take_sums(ITERS, 0)
            divide(ITERS, 0, fill_count(ITERS - 1, len(LAST), LAST) + 1, slot[2])
            dve.wait_ge(norm_done, norm_count(ITERS, 0))
            residual(1)
            link(moments(attn, 1))
            statistics(1)
            link(normalised(attn, 1))
            modulated(1, 3, 4).then_inc(h_ok, 1)
            dve.wait_ge(logit_mm, 1)
            route(1, slot[2])
            split_rows(1)

            def weight(m, at, row):
                for q in range(FCH):
                    n, g = chunk(1, m, q), gat[:, at + q]
                    dve.wait_ge(hid_ok, UPB + n + 1)
                    dve.wait_ge(l2_done, n + 1)
                    if row is None:
                        if q == 0:
                            dve.wait_ge(gat_ok, RING + FALL)
                            dve.wait_ge(filled, BODY * ITERS + 3)
                        ins = v.tensor_copy(g, hid[:, at + q])
                    else:
                        ins = v.tensor_tensor(g, hid[:, at + q], row[:, q * CH:(q + 1) * CH], ALU.mult)
                    ins.then_inc(gat_ok, 1)
                for q in range(FCH):
                    dve.wait_ge(gat_ok, RING + chunk(1, m, q) + 1)
                    v.tensor_copy(gat_hi[:, at + q], gat[:, at + q]).then_inc(ghi_ok, 1)
                dve.wait_ge(ghi_ok, FCH * m + FCH)
                v.tensor_tensor(gat_lo[:, at + 1], gat[:, at + 1], gat_hi[:, at + 1].bitcast(F32),
                                ALU.subtract).then_inc(glo_ok[1], 1)

            def routed(i, k):
                dve.wait_ge(row_ld[k], 16 * (E // 3 + i + 1))
                weight(3 * i + k + 1, place(1, k), cwb[k])

            def output(b, half):
                lo, hi = half * C // HALVES, (half + 1) * C // HALVES
                dve.wait_ge(y_mm, HALVES * b + half + 1)
                v.tensor_tensor(h_sb[:, lo:hi, cols(b)], attn[:, lo:hi, cols(b)],
                                y_sums[b][:].rearrange("m (c d) -> m c d", c=C)[:, lo:hi], ALU.add).then_inc(y_ok, 1)

            weight(0, place(1, -1), None)
            experts(dve, 1, 0, 2, routed)
            output(0, 0)
            experts(dve, 1, 2, 3, routed)
            output(0, 1)
            experts(dve, 1, 3, E // 3, routed)
            for half in range(HALVES):
                output(1, half)

        @block.tensor
        def _(pe):
            mm = nc.tensor.matmul

            def turn(dst, src, lo=0, hi=C):
                for c in range(lo, hi):
                    last = nc.tensor.transpose(dst[:, c * M:(c + 1) * M], src(c), ident[:])
                return last

            pe.sem_inc(l2_done, RING)
            pe.wait_ge(wmp_ok, 1)
            pe.wait_ge(silu_ok, 1)

            for k, w_k in enumerate((wmp[:, 0:D], wmp[:, D:2 * D], wm[:, 5 * D:6 * D])):
                mm(slot[2][:, CH + k * B:CH + (k + 1) * B], w_k, sil[:, 3], start=True, stop=True)

            def spread_modulation(dst, w, n):
                for b in range(B):
                    last = mm(dst.rearrange("p (k b d) -> p k b d", k=n, b=B)[:, :, b], silb[:, b], w,
                              start=True, stop=True)
                return last

            pe.wait_ge(silb_ok, B)
            spread_modulation(acc[:, 0:CH], wmp[:], 2).then_inc(mod_mm, 1)
            spread_modulation(acc[:, CH:T], wm[:, 2 * D:4 * D], 2)
            spread_modulation(slot[2][:, 0:B * D], wm[:, 4 * D:5 * D], 1).then_inc(mod_mm, 1)
            def keep_busy(times):
                for _ in range(times):
                    mm(slot[1][:, 0:128], ones[:], ones[:], start=True, stop=True)

            pe.wait_ge(consts, 2)
            for b in range(B):
                if b:
                    pe.wait_ge(reach_ok, 1)
                    keep_busy(WARM_UP)
                for half in range(HALVES):
                    pe.wait_ge(z_ok, HALVES * b + half + 1)
                    turn(z_slot[b], lambda c: h_sb[:, c, cols(b)], half * C // HALVES,
                         (half + 1) * C // HALVES).then_inc(hT_mm, 1)

            def scores(dst, j, q, c, rows):
                k_c = keys[j][0:rows, q, c * M:(c + 1) * M]
                for half in range(HALVES):
                    lo, hi = half * CH, (half + 1) * CH
                    cuts = [(lo, hi, 1)]
                    if lo <= c * M < hi:
                        cuts = [(lo, c * M, 1), (c * M, (c + 1) * M, 0), ((c + 1) * M, hi, 1)]
                    for a, z, s in cuts:
                        if z > a:
                            last = mm(dst[:, a:z], k_c, qry[j][0:rows, q, s, a:z], start=True, stop=True)
                return last

            exact = exact_wanted(pe)
            with pe.If(exact > 0):
                pe.wait_ge(hT_ok, HALVES * B)
                with pe.Fori(0, NG) as n:
                    pe.wait_ge(ex_ld, 16 * (KEY_LOADS + QUERY_LOADS) * (n + 1))
                    for u in range(G * C):
                        pe.wait_ge(ex_max, G * C * n + u + C - 1)
                        scores(slot[u % 2], 0, u // C, u % C, ROWS).then_inc(ex_mm, 1)
                pe.wait_ge(ex_max, C * HG + C)
                pe.wait_ge(mod_ok, 4)
                for b in range(B):
                    last = nc.tensor.transpose(acc[:, b * 128:(b + 1) * 128],
                                               shift[:, b * H:(b + 1) * H].rearrange("p h c -> p (h c)"), ident[:])
                last.then_inc(shiftT_mm, 1)
                pe.wait_ge(spart_ok, 2)

            def weigh(jv, cp, half):
                for q in range(G):
                    last = mm(acc[32 * q:32 * q + 32, half * CH:(half + 1) * CH], val[jv][:, cp, q, :],
                              prob[cp % 2][:, q, half * CH:(half + 1) * CH], start=cp == 0, stop=cp == C - 1,
                              tile_position=(0, 32 * q))
                last.then_inc(pv_done, 1)

            def logits(b, dst):
                for c in range(C):
                    last = mm(dst[:, 16 * c:16 * c + E], hT[:, b * T + c * M:b * T + (c + 1) * M], rw[:],
                              start=True, stop=True)
                return last

            def turn_weights(b, dst):
                return turn(dst[0:E], lambda c: lg[:, b, 3, c])

            def free_slot(it, r, body):
                p = r - SLOTS
                while p >= 0 and body[p][0] == "none":
                    p -= SLOTS
                if p < 0:
                    if body is FIRST and r == 2:
                        pe.wait_ge(hT_ok, HALVES * B)
                    if body is not FIRST:
                        pe.wait_ge(exp_done, exp_count(it, p + 1))
                    return
                kind, j = body[p][0:2]
                if kind == "turn":
                    pe.wait_ge(norm_done, norm_count(it, j))
                elif kind == "h2T":
                    pe.wait_ge(h2T_ok, 1)
                elif kind == "logit":
                    pe.wait_ge(lsub, 1)
                elif kind == "cwT":
                    pe.wait_ge(cwT_ok, 1)
                else:
                    pe.wait_ge(exp_done, exp_count(it, sum(u[0] == "score" for u in body[:p + 1])))

            def attend(it, body):
                for r, (kind, j, c, q) in enumerate(body):
                    if kind == "none":
                        continue
                    dst = slot[r % SLOTS]
                    free_slot(it, r, body)
                    if kind == "turn":
                        pe.wait_ge(evac, evac_count(it, j, HALVES - 1))
                        turn(dst, lambda c: oT[:, c * M:(c + 1) * M]).then_inc(filled, 1)
                    elif kind == "h2T":
                        pe.wait_ge(h_ok, 1)
                        turn(dst, lambda c: h_sb[:, c, cols(0)]).then_inc(filled, 1)
                    elif kind == "logit":
                        pe.wait_ge(h2T_ok, 1)
                        pe.wait_ge(ld_ffn, 96)
                        logits(0, dst).then_inc(filled, 1)
                    elif kind == "cwT":
                        pe.wait_ge(cw_ok, 1)
                        turn_weights(0, dst).then_inc(filled, 1)
                    if kind != "score":
                        continue
                    if c == 0 and q == 0:
                        pe.wait_ge(opnd[j], 16 * (OPND_LOADS * (it + 1) - (QUERY_LOADS if j == 0 else 0)))
                    if body is FIRST and j == 0 and c == 0 and q % 2 == 0:
                        pe.wait_ge(first_q[q // 2], 16)
                    scores(dst, j, q, c, KROWS).then_inc(filled, 1)
                    step = C * j + c
                    if q % 2 == 1 and not (body is FIRST and step == 0):
                        half, cp, jp = q // 2, (c - 1) % C, j if c else 1 - j
                        if half == 0:
                            pe.wait_ge(exp_done, exp_count(it, G * step))
                            if cp == 0:
                                pe.wait_ge(val_ok[jp], it + 1)
                        if cp == 0 and not (body is FIRST and j == 0):
                            pe.wait_ge(evac, evac_count(it, j, half))
                        weigh(jp, cp, half)

            pe.wait_ge(mod_ok, 4)
            pe.wait_ge(hw_ok, HALVES)
            keep_busy(WARM_UP // 2)
            attend(0, FIRST)
            with pe.Fori(1, ITERS - 1) as it:
                attend(it, MIDDLE)
            attend(ITERS - 1, LAST)
            pe.wait_ge(exp_done, exp_count(ITERS, 0))
            for half in range(HALVES):
                weigh(1, C - 1, half)

            def up(b, m, at, w):
                for q in range(FCH):
                    pe.wait_ge(hid_ok, chunk(b, m, q) + 1)
                    dst, at_q = up_bank[(at + q) % UPB], slice(q * CH, (q + 1) * CH)
                    mm(dst, w[:, 0], hT_hi[b][:, at_q], start=True, stop=False)
                    mm(dst, w[:, 0], hT_lo[b][:, at_q], start=False, stop=False)
                    mm(dst, w[:, 1], hT_hi[b][:, at_q], start=False, stop=True).then_inc(l1_done, 1)

            def down(b, m, at, w, start=False, stop=False):
                def dst(q):
                    return sums[b][:, q * CH:(q + 1) * CH]

                if b == 0:
                    for q in range(FCH):
                        pe.wait_ge(gat_ok, RING + chunk(b, m, q) + 1)
                        mm(dst(q), w[:], gat[:, at + q], start=start, stop=stop).then_inc(l2_done, 1)
                    return
                for q in range(FCH):
                    pe.wait_ge(ghi_ok, FCH * m + q + 1)
                    mm(dst(q), w[:, 0], gat_hi[:, at + q], start=start, stop=False)
                    mm(dst(q), w[:, 1], gat_hi[:, at + q], start=False, stop=False)
                for q in range(FCH):
                    pe.wait_ge(glo_ok[q], m + 1)
                    mm(dst(q), w[:, 0], gat_lo[:, at + q], start=False, stop=stop).then_inc(l2_done, 1)

            def loaded(b, i, k):
                pe.wait_ge(w1_ok, E * b + 3 * i + k + 1)

            def routed(b, i, k, last=False):
                if not last:
                    k1, i1 = (k + 1) % 3, i + (k + 1) // 3
                    loaded(b, i1, k1)
                    up(b, 3 * i + k + 2, place(b, k1), w1r[k1])
                else:
                    second_biases(b)
                if b:
                    pe.wait_ge(w2_ok, 3 * i + k + 2)
                else:
                    pe.wait_ge(w2_ld[k], 16 * (i + 1))
                down(b, 3 * i + k + 1, place(b, k), (w2r if b else w2)[k], stop=last)

            def second_biases(b):
                for q in range(FCH):
                    mm(sums[b][:, q * CH:(q + 1) * CH], b2r[:], cwT[:, b, q * CH:(q + 1) * CH], start=False, stop=False)

            pe.wait_ge(h2s_ok, 1)
            pe.wait_ge(ws1_ok, 1)
            pe.wait_ge(ld_ffn, 96)
            up(0, 0, place(0, -1), ws1r)
            pe.wait_ge(evac, evac_count(ITERS, 0, HALVES - 1))
            turn(slot[2], lambda c: oT[:, c * M:(c + 1) * M]).then_inc(filled, 1)
            loaded(0, 0, 0)
            up(0, 1, place(0, 0), w1r[0])
            down(0, 0, place(0, -1), ws2, start=True)
            experts(pe, 0, 0, 2, lambda i, k: routed(0, i, k))
            pe.wait_ge(h_ok, 2)
            turn(slot[2], lambda c: h_sb[:, c, cols(1)]).then_inc(h2T_mm, 1)
            experts(pe, 0, 2, 3, lambda i, k: routed(0, i, k))
            pe.wait_ge(h2T_ok, 2)
            logits(1, slot[2]).then_inc(logit_mm, 1)
            experts(pe, 0, 3, 4, lambda i, k: routed(0, i, k))
            pe.wait_ge(cw_ok, 2)
            turn_weights(1, slot[2]).then_inc(cwT_mm, 1)
            experts(pe, 0, 4, 5, lambda i, k: routed(0, i, k, last=k == 2))

            pe.wait_ge(h2s_ok, 2)
            up(1, 0, place(1, -1), ws1r)
            loaded(1, 0, 0)
            up(1, 1, place(1, 0), w1r[0])
            pe.wait_ge(cwT_ok, 2)
            pe.wait_ge(w2_ok, 1)
            down(1, 0, place(1, -1), ws2r, start=True)
            experts(pe, 1, 0, 1, lambda i, k: routed(1, i, k))

            def back(b):
                for half in range(HALVES):
                    pe.wait_ge(ffT_ok, FCH * b + half + 1)
                    turn(y_sums[b], lambda c: hT[:, b * T + c * M:b * T + (c + 1) * M], half * C // HALVES,
                         (half + 1) * C // HALVES).then_inc(y_mm, 1)

            pe.wait_ge(ffT_ok, FCH)
            back(0)
            experts(pe, 1, 1, E // 3 - 1, lambda i, k: routed(1, i, k))
            experts(pe, 1, E // 3 - 1, E // 3, lambda i, k: routed(1, i, k, last=k == 2))
            pe.wait_ge(hid_ok, UPB + 2 * FALL)
            back(1)


_INS = ["L0_attn_x", "L0_attn_inter_palace_weight", "L0_ffn_router_W", "L0_ffn_router_b", "L0_ffn_sW1",
        "L0_ffn_sb1", "L0_ffn_sW2", "L0_ffn_sb2", "L0_ffn_eW1", "L0_ffn_eb1", "L0_ffn_eW2", "L0_ffn_eb2",
        "L0_c", "L0_wmod"]


def kernel(**inputs):
    import numpy as np
    import concourse.bacc as bacc
    from concourse.bass_utils import run_bass_kernel_spmd

    nc = bacc.Bacc("TRN2", target_bir_lowering=False, num_devices=1)
    arrays, args = {}, []
    for name in _INS:
        a = np.ascontiguousarray(inputs[name])
        if a.ndim == 0:
            a = a.reshape(1)
        arrays[f"in_{name}"] = a
        args.append(nc.dram_tensor(f"in_{name}", a.shape, mybir.dt.from_np(a.dtype), kind="ExternalInput").ap())
    out = nc.dram_tensor("out", (B, T, D), F32, kind="ExternalOutput").ap()
    adaln_block(nc, *args, out)
    r = run_bass_kernel_spmd(nc, [arrays], core_ids=[0])
    return r.results[0]["out"]
```
